# Optimizing a Trainium2 kernel written in Bass

```python
import numpy as np
import jax
import jax.numpy as jnp

def _softmax(x, axis=-1):
    return jax.nn.softmax(x, axis=axis)

def _gelu(x):
    return jax.nn.gelu(x, approximate=True)

def _silu(x):
    return jax.nn.silu(x)

def _sigmoid(x):
    return jax.nn.sigmoid(x)

def _layernorm(x, axis=-1, eps=1e-05):
    m = jnp.mean(x, axis=axis, keepdims=True)
    v = jnp.var(x, axis=axis, keepdims=True)
    return (x - m) / jnp.sqrt(v + eps)

def _scatter_add(tgt, idx, src, axis=0):
    return tgt.at[idx].add(src)

def _segment_sum(src, seg, n):
    return jax.ops.segment_sum(src, seg, n)
kernel_name = 'mk_macaron_d1_jaxref_r8_7c1611'

def setup_inputs(seed: int=0):
    np.random.seed(seed)
    _w = jnp.asarray

    def _L0_attn_setup():
        import jax, jax.numpy as jnp
        import numpy as np
        import math
        DIM = 128
        HEADS = 16
        HEAD_DIM = DIM // HEADS
        FFN_DIM = 512
        WINDOW = 125
        B, T = (2, 256)

        def _layernorm(x, w, b, eps=1e-05):
            mu = jnp.mean(x, axis=-1, keepdims=True)
            var = jnp.var(x, axis=-1, keepdims=True)
            return (x - mu) / jnp.sqrt(var + eps) * w + b

        def _rotate_half(x):
            x1, x2 = jnp.split(x, 2, axis=-1)
            return jnp.concatenate([-x2, x1], axis=-1)

        def _rope_tables(seq_len, dim, theta=10000.0):
            inv_freq = 1.0 / theta ** (jnp.arange(0, dim, 2, dtype=jnp.float32) / dim)
            t = jnp.arange(seq_len, dtype=jnp.float32)
            freqs = jnp.outer(t, inv_freq)
            emb = jnp.concatenate([freqs, freqs], axis=-1)
            return (jnp.cos(emb), jnp.sin(emb))

        def _block(x, norm1_w, norm1_b, norm2_w, norm2_b, wq, wk, wv, wo, w1, b1, w2, b2, ls1, ls2):
            Bx, Tx, D = x.shape
            h = _layernorm(x, norm1_w, norm1_b)

            def proj(w):
                y = jnp.einsum('btd,ed->bte', h, w)
                return y.reshape(Bx, Tx, HEADS, HEAD_DIM).transpose(0, 2, 1, 3)
            Q, K, V = (proj(wq), proj(wk), proj(wv))
            cos, sin = _rope_tables(Tx, HEAD_DIM)
            cos = cos[None, None]
            sin = sin[None, None]
            Q = Q * cos + _rotate_half(Q) * sin
            K = K * cos + _rotate_half(K) * sin
            idx = jnp.arange(Tx)
            diff = idx[:, None] - idx[None, :]
            mask = jnp.where((diff >= 0) & (diff < WINDOW), 0.0, -jnp.inf)
            scale = math.sqrt(HEAD_DIM)
            scores = jnp.einsum('bhtd,bhsd->bhts', Q, K) / scale + mask[None, None]
            attn = jax.nn.softmax(scores, axis=-1)
            attn_out = jnp.einsum('bhts,bhsd->bhtd', attn, V)
            attn_out = attn_out.transpose(0, 2, 1, 3).reshape(Bx, Tx, D)
            x = x + jnp.einsum('btd,ed->bte', attn_out, wo) * ls1
            h2 = _layernorm(x, norm2_w, norm2_b)
            f = jax.nn.gelu(jnp.einsum('btd,fd->btf', h2, w1) + b1, approximate=False)
            f = jnp.einsum('btf,df->btd', f, w2) + b2
            x = x + f * ls2
            return x
        key = jax.random.key(seed)
        ks = jax.random.split(key, 12)
        s = 0.02
        return {'x': jax.random.normal(ks[0], (B, T, DIM), dtype=jnp.float32), 'norm1_w': jnp.ones((DIM,), jnp.float32), 'norm1_b': jnp.zeros((DIM,), jnp.float32), 'norm2_w': jnp.ones((DIM,), jnp.float32), 'norm2_b': jnp.zeros((DIM,), jnp.float32), 'wq': jax.random.normal(ks[1], (DIM, DIM), jnp.float32) * s, 'wk': jax.random.normal(ks[2], (DIM, DIM), jnp.float32) * s, 'wv': jax.random.normal(ks[3], (DIM, DIM), jnp.float32) * s, 'wo': jax.random.normal(ks[4], (DIM, DIM), jnp.float32) * s, 'w1': jax.random.normal(ks[5], (FFN_DIM, DIM), jnp.float32) * s, 'b1': jnp.zeros((FFN_DIM,), jnp.float32), 'w2': jax.random.normal(ks[6], (DIM, FFN_DIM), jnp.float32) * s, 'b2': jnp.zeros((DIM,), jnp.float32), 'ls1': jnp.full((DIM,), 0.01, jnp.float32), 'ls2': jnp.full((DIM,), 0.01, jnp.float32)}
    _L0_attn_in = _L0_attn_setup()

    def _L0_ffn_setup():
        import jax, jax.numpy as jnp
        import numpy as np
        DIM = 128
        HIDDEN = 384
        SCALE = 1.0 / 127.0

        def _dequant(w_int, dtype):
            return w_int.astype(dtype) * jnp.asarray(SCALE, dtype)
        key = jax.random.key(seed)
        k_x, k_g, k_u, k_d = jax.random.split(key, 4)
        x = jax.random.normal(k_x, (4, 256, DIM), dtype=jnp.float32)
        w_gate = jax.random.randint(k_g, (HIDDEN, DIM), -127, 128, dtype=jnp.int32)
        w_up = jax.random.randint(k_u, (HIDDEN, DIM), -127, 128, dtype=jnp.int32)
        w_down = jax.random.randint(k_d, (DIM, HIDDEN), -127, 128, dtype=jnp.int32)
        return {'x': x, 'w_gate': w_gate, 'w_up': w_up, 'w_down': w_down}
    _L0_ffn_in = _L0_ffn_setup()
    _d = {'L0_attn_x': _L0_attn_in['x'], 'L0_attn_norm1_w': _L0_attn_in['norm1_w'], 'L0_attn_norm1_b': _L0_attn_in['norm1_b'], 'L0_attn_norm2_w': _L0_attn_in['norm2_w'], 'L0_attn_norm2_b': _L0_attn_in['norm2_b'], 'L0_attn_wq': _L0_attn_in['wq'], 'L0_attn_wk': _L0_attn_in['wk'], 'L0_attn_wv': _L0_attn_in['wv'], 'L0_attn_wo': _L0_attn_in['wo'], 'L0_attn_w1': _L0_attn_in['w1'], 'L0_attn_b1': _L0_attn_in['b1'], 'L0_attn_w2': _L0_attn_in['w2'], 'L0_attn_b2': _L0_attn_in['b2'], 'L0_attn_ls1': _L0_attn_in['ls1'], 'L0_attn_ls2': _L0_attn_in['ls2'], 'L0_ffn_w_gate': _L0_ffn_in['w_gate'], 'L0_ffn_w_up': _L0_ffn_in['w_up'], 'L0_ffn_w_down': _L0_ffn_in['w_down']}
    _x0 = _d['L0_attn_x']
    _d['L0_attn_x'] = jax.random.normal(jax.random.fold_in(jax.random.key(seed), 1), (32, 256, 128), dtype=_x0.dtype)
    del _x0
    return _d

def reference(L0_attn_x, L0_attn_norm1_w, L0_attn_norm1_b, L0_attn_norm2_w, L0_attn_norm2_b, L0_attn_wq, L0_attn_wk, L0_attn_wv, L0_attn_wo, L0_attn_w1, L0_attn_b1, L0_attn_w2, L0_attn_b2, L0_attn_ls1, L0_attn_ls2, L0_ffn_w_gate, L0_ffn_w_up, L0_ffn_w_down):

    def _L0_attn_ref(x, norm1_w, norm1_b, norm2_w, norm2_b, wq, wk, wv, wo, w1, b1, w2, b2, ls1, ls2):
        import jax, jax.numpy as jnp
        import numpy as np
        import math
        DIM = 128
        HEADS = 16
        HEAD_DIM = DIM // HEADS
        FFN_DIM = 512
        WINDOW = 125
        B, T = (2, 256)

        def _layernorm(x, w, b, eps=1e-05):
            mu = jnp.mean(x, axis=-1, keepdims=True)
            var = jnp.var(x, axis=-1, keepdims=True)
            return (x - mu) / jnp.sqrt(var + eps) * w + b

        def _rotate_half(x):
            x1, x2 = jnp.split(x, 2, axis=-1)
            return jnp.concatenate([-x2, x1], axis=-1)

        def _rope_tables(seq_len, dim, theta=10000.0):
            inv_freq = 1.0 / theta ** (jnp.arange(0, dim, 2, dtype=jnp.float32) / dim)
            t = jnp.arange(seq_len, dtype=jnp.float32)
            freqs = jnp.outer(t, inv_freq)
            emb = jnp.concatenate([freqs, freqs], axis=-1)
            return (jnp.cos(emb), jnp.sin(emb))

        def _block(x, norm1_w, norm1_b, norm2_w, norm2_b, wq, wk, wv, wo, w1, b1, w2, b2, ls1, ls2):
            Bx, Tx, D = x.shape
            h = _layernorm(x, norm1_w, norm1_b)

            def proj(w):
                y = jnp.einsum('btd,ed->bte', h, w)
                return y.reshape(Bx, Tx, HEADS, HEAD_DIM).transpose(0, 2, 1, 3)
            Q, K, V = (proj(wq), proj(wk), proj(wv))
            cos, sin = _rope_tables(Tx, HEAD_DIM)
            cos = cos[None, None]
            sin = sin[None, None]
            Q = Q * cos + _rotate_half(Q) * sin
            K = K * cos + _rotate_half(K) * sin
            idx = jnp.arange(Tx)
            diff = idx[:, None] - idx[None, :]
            mask = jnp.where((diff >= 0) & (diff < WINDOW), 0.0, -jnp.inf)
            scale = math.sqrt(HEAD_DIM)
            scores = jnp.einsum('bhtd,bhsd->bhts', Q, K) / scale + mask[None, None]
            attn = jax.nn.softmax(scores, axis=-1)
            attn_out = jnp.einsum('bhts,bhsd->bhtd', attn, V)
            attn_out = attn_out.transpose(0, 2, 1, 3).reshape(Bx, Tx, D)
            x = x + jnp.einsum('btd,ed->bte', attn_out, wo) * ls1
            h2 = _layernorm(x, norm2_w, norm2_b)
            f = jax.nn.gelu(jnp.einsum('btd,fd->btf', h2, w1) + b1, approximate=False)
            f = jnp.einsum('btf,df->btd', f, w2) + b2
            x = x + f * ls2
            return x
        return _block(x, norm1_w, norm1_b, norm2_w, norm2_b, wq, wk, wv, wo, w1, b1, w2, b2, ls1, ls2)

    def _L0_ffn_ref(x, w_gate, w_up, w_down):
        import jax, jax.numpy as jnp
        import numpy as np
        DIM = 128
        HIDDEN = 384
        SCALE = 1.0 / 127.0

        def _dequant(w_int, dtype):
            return w_int.astype(dtype) * jnp.asarray(SCALE, dtype)
        wg = _dequant(w_gate, x.dtype)
        wu = _dequant(w_up, x.dtype)
        wd = _dequant(w_down, x.dtype)
        gate = jnp.einsum('bsd,hd->bsh', x, wg)
        up = jnp.einsum('bsd,hd->bsh', x, wu)
        h = jax.nn.silu(gate) * up
        return jnp.einsum('bsh,dh->bsd', h, wd)
    x = L0_attn_x
    x = x + 0.5 * _L0_ffn_ref(_layernorm(x, axis=-1), L0_ffn_w_gate, L0_ffn_w_up, L0_ffn_w_down)
    x = x + _L0_attn_ref(_layernorm(x, axis=-1), L0_attn_norm1_w, L0_attn_norm1_b, L0_attn_norm2_w, L0_attn_norm2_b, L0_attn_wq, L0_attn_wk, L0_attn_wv, L0_attn_wo, L0_attn_w1, L0_attn_b1, L0_attn_w2, L0_attn_b2, L0_attn_ls1, L0_attn_ls2)
    x = x + 0.5 * _L0_ffn_ref(_layernorm(x, axis=-1), L0_ffn_w_gate, L0_ffn_w_up, L0_ffn_w_down)
    return x

_drawn_inputs = setup_inputs


def setup_inputs(seed=0):
    import zlib

    import numpy as np

    out = dict(_drawn_inputs(seed))
    spreads = {'L0_attn_norm1_w': (1.0, 0.6),
     'L0_attn_norm1_b': (0.0, 2.0),
     'L0_attn_norm2_w': (1.0, 0.6),
     'L0_attn_norm2_b': (0.0, 2.0),
     'L0_attn_b1': (0.0, 2.0),
     'L0_attn_b2': (0.0, 2.0),
     'L0_attn_ls1': (0.009999999776482582, 0.6),
     'L0_attn_ls2': (0.009999999776482582, 0.6)}
    factors = {'L0_attn_wq': 64.0,
     'L0_attn_wk': 64.0,
     'L0_attn_wv': 64.0,
     'L0_attn_wo': 64.0,
     'L0_attn_w1': 64.0,
     'L0_attn_w2': 64.0}
    for name, (base, spread) in spreads.items():
        noise = np.random.default_rng([zlib.crc32(name.encode()), seed]).standard_normal(out[name].shape)
        drawn = base * np.exp(spread * noise) if base else spread * noise
        out[name] = jnp.asarray(drawn.astype(out[name].dtype))
    for name, factor in factors.items():
        out[name] = (out[name] * factor).astype(out[name].dtype)
    return out
```

```python
from contextlib import ExitStack

import numpy as np
import concourse.bass as bass
from concourse import mybir
from concourse.alu_op_type import AluOpType as ALU

ACT = mybir.ActivationFunctionType
AX = mybir.AxisListType
F32 = mybir.dt.float32
BF16 = mybir.dt.bfloat16
I32 = mybir.dt.int32

P = 128
B, T, D = 32, 256, 128
H, HD = 16, 8
FF, HID = 512, 384
WINDOW = 125
EPS = 1e-5
SCALE = float(np.float32(1.0 / 127.0))
NT = 4
PAIRS = B * T // (NT * P)
TOK = NT * P
QUAD = 4
GROUPS = 2 * H // QUAD
CH, CF = HID // P, FF // P

STK = 64
MCOL = 32
MASKED = -1e30

ATTN, BACK, FRONT = "attn", "back", "front"
ORDER = (
    ("qkv", 0), ("oT", 0), ("split", 0), ("wo", 0), ("stackT", 0), ("ln_a", "gelu"), ("max", 0), ("ln_b", "gelu"), ("max", 1), ("nm", 0),
    ("w1", 0), ("max", 2), ("q2T", 0), ("main", 0), ("gelu", 0), ("w1", 2), ("max", 3), ("nm", 1),
    ("pv", 0), ("w2", 0), ("main", 1), ("norm", 0), ("ln_a", "ffn2"), ("q2T", 1), ("qkv", 1), ("ln_b", "ffn2"),
    ("pv", 1), ("main", 2), ("split", 1), ("gate", ("ffn2", 0)), ("norm", 1), ("gate", ("ffn2", 1)),
    ("pv", 2), ("main", 3), ("gate", ("ffn2", 2)), ("norm", 2), ("stackT", 1), ("down", "ffn2"),
    ("hand", 0), ("max", 4), ("ln_a", "ffn1"), ("pv", 3), ("max", 5), ("nm", 2), ("ln_b", "ffn1"), ("norm", 3), ("max", 6), ("q2T", 2), ("main", 4),
    ("gate", ("ffn1", 0)), ("gate", ("ffn1", 1)), ("max", 7), ("nm", 3), ("pv", 4), ("main", 5), ("gate", ("ffn1", 2)), ("q2T", 3),
    ("norm", 4), ("down", "ffn1"), ("pv", 5), ("main", 6), ("ln_a", "attn"),
    ("norm", 5), ("ln_b", "attn"), ("pv", 6), ("main", 7), ("norm", 6), ("pv", 7), ("norm", 7),
)
STAGE = {"qkv": ATTN, "split": ATTN, "stackT": ATTN, "max": ATTN, "nm": ATTN, "q2T": ATTN, "main": ATTN, "pv": ATTN, "norm": ATTN,
         "oT": BACK, "wo": BACK, "w1": BACK, "gelu": BACK, "w2": BACK, "hand": ATTN}


def stage_of(name, arg):
    if name in STAGE:
        return STAGE[name]
    block = arg[0] if isinstance(arg, tuple) else arg
    return FRONT if block in ("ffn1", "attn") else BACK


X_TAKES = {"qkv": 2, "stackT": 4, "max": 3, "q2T": 1}
X_FIRST, X_USES = {}, 0
for _part in ORDER:
    if _part[0] in X_TAKES:
        X_FIRST[_part] = X_USES
        X_USES += X_TAKES[_part[0]]
assert X_USES % 2 == 0


def heads_of(g):
    s, j = g // 4, g % 4
    first = 8 * (j // 2) + j % 2
    return s, slice(first, first + 7, 2), slice(STK * (j % 2), STK * (j % 2) + STK)


class Count:

    def __init__(self, sem, per):
        self.sem, self.per = sem, per

    def of(self, pair, n=None):
        value = pair * self.per + (self.per if n is None else n)
        return max(value, 0) if isinstance(value, int) else value


def build(nc, a):
    with ExitStack() as ctx:
        def sb(name, shape, dt=F32):
            return ctx.enter_context(nc.sbuf_tensor(name, shape, dt))

        def bank(name):
            return ctx.enter_context(nc.psum_tensor(name, [P, 512], F32))

        def count(name, per=1):
            return Count(ctx.enter_context(nc.semaphore(name)), per)

        ident = sb("ident", [P, P])
        identb = sb("identb", [P, P], BF16)
        mask_max = sb("mask_max", [P, 2, 512], BF16)
        mask_main = sb("mask_main", [P, 2, 512], BF16)
        cosr = sb("cosr", [P, 2, 2 * D])
        sinr = sb("sinr", [P, 2, 2 * D])
        wqkv = sb("wqkv", [P, 3 * D])
        wo = sb("wo", [P, D])
        w1 = sb("w1", [P, FF])
        w2 = sb("w2", [P, CF, D])
        gate_i = sb("gate_i", [P, HID], I32)
        up_i = sb("up_i", [P, HID], I32)
        down_i = sb("down_i", [P, CH * D], I32)
        wgate = sb("wgate", [P, HID])
        wup = sb("wup", [P, HID])
        wdown = sb("wdown", [P, CH, D])
        cols = sb("cols", [P, 4 + CF])
        rows = sb("rows", [P, 3, D])
        b2l = sb("b2l", [P, D])
        mhalf = sb("mhalf", [P, NT])

        x_in = sb("x_in", [P, NT, D])
        x1 = sb("x1", [P, NT, D])
        u = sb("u", [P, NT, D])
        x1b = sb("x1b", [P, NT, D])
        u_back = sb("u_back", [P, NT, D])
        x1b_back = sb("x1b_back", [P, NT, D])
        u2 = sb("u2", [P, NT, D])
        ux = sb("ux", [P, NT, D])
        x2 = sb("x2", [P, NT, D])
        xout = sb("xout", [P, NT, D])
        stats = sb("stats", [P, NT, 6])
        mv = sb("mv", [P, NT, 2])
        lnv = sb("lnv", [P, 4, NT])
        rstd = sb("rstd", [P, 2, NT])
        lnr = sb("lnr", [P, NT])
        xn = sb("xn", [P, NT, D])
        hT = sb("hT", [P, TOK])
        hqT = sb("hqT", [P, TOK])
        th = sb("th", [P, TOK])
        sg = sb("sg", [P, TOK])
        act = sb("act", [P, CF, TOK])

        rot1 = sb("rot1", [P, 2, 2 * D])
        rot2 = sb("rot2", [P, 2, 2 * D])
        r = sb("r", [P, 2, 2 * D])
        e1 = sb("e1", [P, 2, 2 * D])
        part1 = sb("part1", [P, 2, 2 * D], BF16)
        part2 = sb("part2", [P, 2, 2 * D], BF16)
        part3 = sb("part3", [P, 2, 2 * D], BF16)
        qs = sb("qs", [P, 2, 2 * H, STK], BF16)
        ks = sb("ks", [P, 2, 2 * H, STK], BF16)
        vs = sb("vs", [P, 2, 2 * H, 32])
        qT = sb("qT", [P, 2, H // 2, T], BF16)
        kT = sb("kT", [P, 2, H // 2, T], BF16)
        q2T = sb("q2T", [P, 2, 4, T], BF16)
        nmax = sb("nmax", [P, 2, 2, H])
        nme = sb("nme", [P, 2, 8])
        pT = sb("pT", [P, 2, 3, 512])
        oq = sb("oq", [P, T])
        rden = sb("rden", [P, 2 * QUAD])
        on = sb("on", [P, NT, D])
        oT = sb("oT", [P, TOK])

        bx = [bank("bx0"), bank("bx1")]
        bm = [bank("bm0"), bank("bm1")]
        bo = bank("bo")
        bt = bank("bt")
        bg, bu = bank("bg"), bank("bu")

        loaded = count("loaded")
        consts_done = count("consts_done")
        stacks_set = count("stacks_set")
        x_loaded = count("x_loaded", 16)
        out_stored = count("out_stored", 16)
        LN = ("ffn1", "attn", "gelu", "ffn2")
        bn_done = {b: count(f"bn_{b}") for b in LN}
        mv_done = {b: count(f"mv_{b}") for b in LN}
        rs_done = {b: count(f"rs_{b}", 6 if b == "attn" else 2) for b in LN}
        xn_done = {b: count(f"xn_{b}") for b in LN}
        xt_done = {b: count(f"xt_{b}") for b in LN}
        ht_done = {b: count(f"ht_{b}") for b in LN}
        FFN = ("ffn1", "ffn2")
        gate_done = {b: count(f"gate_{b}", CH) for b in FFN}
        up_done = {b: count(f"up_{b}", CH) for b in FFN}
        tanh_done = {b: count(f"tanh_{b}", CH) for b in FFN}
        sg_done = {b: count(f"sg_{b}", CH) for b in FFN}
        mul_done = {b: count(f"mul_{b}", CH) for b in FFN}
        down_done = {b: count(f"down_{b}") for b in FFN}
        lnr_done = count("lnr_done")
        x1_done = count("x1_done")
        u_done = count("u_done", 2)
        handed = count("handed", 2)
        ot_tr = count("ot_tr")
        ot_done = count("ot_done")
        wo_done = count("wo_done")
        u2_done = count("u2_done")
        ux_done = count("ux_done")
        w1_done = count("w1_done", CF)
        gelu_done = count("gelu_done", CF)
        w2_done = count("w2_done")
        x2_done = count("x2_done")
        out_done = count("out_done")
        x_full = count("x_full", X_USES)
        x_free = count("x_free", X_USES)
        rot_done = count("rot_done", NT)
        r_done = count("r_done", NT)
        p1_done = count("p1_done", 2)
        e1_done = count("e1_done", 2)
        p2_done = count("p2_done", 2)
        p3_done = count("p3_done", 2)
        stack_done = count("stack_done", 2)
        nm_clear = count("nm_clear", 2)
        nm_done = count("nm_done", 4 * GROUPS // 2)
        m_full = count("m_full", 3 * GROUPS)
        m_free = count("m_free", 3 * GROUPS)
        pv_done = count("pv_done", GROUPS)
        oq_done = count("oq_done", GROUPS)
        oqt_done = count("oqt_done", GROUPS)
        rden_done = count("rden_done", GROUPS)
        on_done = count("on_done", GROUPS)

        pool_passed = count("pool_passed")
        vector_passed = count("vector_passed")

        def walk(eng, part, first=None, last=None):
            def step(k, stages):
                for name, arg in ORDER:
                    stage = stage_of(name, arg)
                    if stage in stages:
                        part(name, arg, k if stage == ATTN else k - 1 if stage == BACK else k + 1)
            step(-1, (FRONT,))
            step(0, (ATTN, FRONT))
            with eng.Fori(1, PAIRS - 1) as k:
                step(k, (ATTN, BACK, FRONT))
            step(PAIRS - 1, (ATTN, BACK))
            step(PAIRS, (BACK,))

        block = ctx.enter_context(nc.Block())

        x_view = a["x"].rearrange("(i t p) d -> i p t d", t=NT, p=P)
        out_view = a["out"].rearrange("(i t p) d -> i p t d", t=NT, p=P)
        LOADS = [(ident, "ident"), (identb, "identb"), (gate_i, "w_gate"), (up_i, "w_up"), (down_i, "w_down"),
                 (cols, "cols"), (rows, "rows"), (wqkv, "wqkv"), (cosr, "cos"), (sinr, "sin"),
                 (mask_max, "mask_max"), (mask_main, "mask_main"), (wo, "wo"), (w1, "w1"), (w2, "w2")]

        @block.sync
        def _(sp):
            def load_x(i):
                sp.wait_ge(x1_done.sem, x1_done.of(i - 1))
                sp.dma_start(x_in[:], x_view[i]).then_inc(x_loaded.sem, 16)

            def store(i):
                sp.wait_ge(out_done.sem, out_done.of(i))
                sp.dma_start(out_view[i], xout[:]).then_inc(out_stored.sem, 16)

            load_x(0)
            for tile, name in LOADS:
                sp.dma_start(tile[:], a[name]).then_inc(loaded.sem, 16)
            load_x(1)
            with sp.Fori(1, PAIRS - 1) as k:
                load_x(k + 1)
                store(k - 1)
            store(PAIRS - 2)
            store(PAIRS - 1)
            sp.wait_ge(out_stored.sem, 16 * PAIRS)

        @block.gpsimd
        def _(pool):
            pool.memset(mhalf[:], -0.5)
            pool.memset(qs[:], 0.0)
            pool.memset(ks[:], 0.0)
            pool.memset(vs[:], 0.0).then_inc(stacks_set.sem, 1)
            pool.wait_ge(stacks_set.sem, 1)
            for s in range(2):
                pool.memset(ks[:, s, :, MCOL:MCOL + 3], 1.0)
                pool.memset(vs[:, s, :, HD:HD + 1], 1.0).then_inc(stacks_set.sem, 1)
            pool.wait_ge(consts_done.sem, 7)

            def part(name, arg, i):
                if name == "ln_a":
                    rs = rs_done[arg]
                    n = 0

                    def op(ins):
                        nonlocal n
                        n += 1
                        ins.then_inc(rs.sem, 1)

                    pool.wait_ge(mv_done[arg].sem, mv_done[arg].of(i))
                    pool.sem_inc(pool_passed.sem, 1)
                    op(pool.tensor_scalar(lnv[:, 0], mv[:, :, 1], EPS, None, ALU.add))
                    pool.wait_ge(rs.sem, rs.of(i, n))
                    pool.sem_inc(pool_passed.sem, 1)
                    if arg != "attn":
                        op(pool.tensor_tensor(rstd[:, 0], lnv[:, 0], mhalf[:], ALU.pow))
                        return
                    op(pool.tensor_tensor(rstd[:, 1], lnv[:, 0], mhalf[:], ALU.pow))
                    pool.wait_ge(rs.sem, rs.of(i, n))
                    pool.sem_inc(pool_passed.sem, 1)
                    op(pool.tensor_tensor(lnv[:, 1], mv[:, :, 1], rstd[:, 1], ALU.mult))
                    pool.wait_ge(rs.sem, rs.of(i, n))
                    pool.sem_inc(pool_passed.sem, 1)
                    op(pool.tensor_tensor(lnv[:, 2], lnv[:, 1], rstd[:, 1], ALU.mult))
                    pool.wait_ge(rs.sem, rs.of(i, n))
                    pool.sem_inc(pool_passed.sem, 1)
                    op(pool.tensor_scalar(lnv[:, 3], lnv[:, 2], EPS, None, ALU.add))
                    pool.wait_ge(rs.sem, rs.of(i, n))
                    pool.sem_inc(pool_passed.sem, 1)
                    op(pool.tensor_tensor(rstd[:, 0], lnv[:, 3], mhalf[:], ALU.pow))
                elif name == "ln_b" and arg == "attn":
                    pool.wait_ge(handed.sem, handed.of(i - 1))
                    pool.sem_inc(pool_passed.sem, 1)
                    for t in range(NT):
                        pool.tensor_tensor(x1b[:, t], x1[:, t], b2l[:], ALU.add)
                    for t in range(NT):
                        ins = pool.tensor_scalar(u[:, t], x1[:, t], mv[:, t, 0:1], rstd[:, 1, t:t + 1],
                                                 ALU.subtract, ALU.mult)
                    ins.then_inc(u_done.sem, 2)
                elif name == "hand":
                    pool.wait_ge(u_done.sem, u_done.of(i))
                    pool.sem_inc(pool_passed.sem, 1)
                    pool.wait_ge(u2_done.sem, u2_done.of(i - 1))
                    pool.sem_inc(pool_passed.sem, 1)
                    pool.wait_ge(ux_done.sem, ux_done.of(i - 1))
                    pool.sem_inc(pool_passed.sem, 1)
                    pool.tensor_copy(u_back[:], u[:]).then_inc(handed.sem, 1)
                    pool.tensor_copy(x1b_back[:], x1b[:]).then_inc(handed.sem, 1)
                elif name == "wo":
                    pool.wait_ge(handed.sem, handed.of(i))
                    pool.sem_inc(pool_passed.sem, 1)
                    pool.wait_ge(u2_done.sem, u2_done.of(i))
                    pool.sem_inc(pool_passed.sem, 1)
                    pool.wait_ge(x2_done.sem, x2_done.of(i - 1))
                    pool.sem_inc(pool_passed.sem, 1)
                    pool.tensor_tensor(ux[:], u2[:], x1b_back[:], ALU.add).then_inc(ux_done.sem, 1)
                elif name == "qkv":
                    for t in range(2):
                        n = 2 * arg + t + 1
                        pool.wait_ge(rot_done.sem, rot_done.of(i, n))
                        pool.sem_inc(pool_passed.sem, 1)
                        if t == 0:
                            pool.wait_ge(p3_done.sem, p3_done.of(i, arg))
                            pool.sem_inc(pool_passed.sem, 1)
                        pool.tensor_tensor(r[:, :, t * D:(t + 1) * D],
                                           rot1[:, t].rearrange("p (a c) -> p a c", a=2),
                                           rot2[:, t].rearrange("p (a c) -> p a c", a=2), ALU.add).then_inc(r_done.sem, 1)
                elif name == "split":
                    s = arg
                    pool.wait_ge(p1_done.sem, p1_done.of(i, s + 1))
                    pool.sem_inc(pool_passed.sem, 1)
                    pool.tensor_tensor(e1[:], r[:], part1[:], ALU.subtract).then_inc(e1_done.sem, 1)
                    pool.wait_ge(p2_done.sem, p2_done.of(i, s + 1))
                    pool.sem_inc(pool_passed.sem, 1)
                    pool.wait_ge(stack_done.sem, stack_done.of(i, s))
                    pool.sem_inc(pool_passed.sem, 1)
                    pool.tensor_tensor(part3[:], e1[:], part2[:], ALU.subtract).then_inc(p3_done.sem, 1)
                    pool.wait_ge(x_full.sem, x_full.of(i - 1, X_FIRST["q2T", 2 * s + 1] + 1))
                    pool.sem_inc(pool_passed.sem, 1)
                    pool.memset(qs[:, s, :, MCOL:MCOL + 3], 0.0).then_inc(nm_clear.sem, 1)
                elif name == "nm":
                    o, s = arg, arg // 2
                    pool.wait_ge(x_free.sem, x_free.of(i, X_FIRST["max", 2 * o + 1] + 3))
                    pool.sem_inc(pool_passed.sem, 1)
                    pool.wait_ge(x_full.sem, x_full.of(i, X_FIRST["stackT", s] + 4))
                    pool.sem_inc(pool_passed.sem, 1)
                    hs = slice(8 * (o % 2), 8 * (o % 2) + 8)
                    nm = nmax[:, s, :, hs]
                    to = [qs[:, s, :, MCOL + c].rearrange("p (t h) -> p t h", t=2)[:, :, hs] for c in range(3)]
                    pool.tensor_copy(to[0], nm).then_inc(nm_done.sem, 1)
                    pool.wait_ge(nm_done.sem, nm_done.of(i, 4 * o + 1))
                    pool.sem_inc(pool_passed.sem, 1)
                    pool.tensor_tensor(nme[:], nm, to[0], ALU.subtract).then_inc(nm_done.sem, 1)
                    pool.wait_ge(nm_done.sem, nm_done.of(i, 4 * o + 2))
                    pool.sem_inc(pool_passed.sem, 1)
                    pool.tensor_copy(to[1], nme[:]).then_inc(nm_done.sem, 1)
                    pool.wait_ge(nm_done.sem, nm_done.of(i, 4 * o + 3))
                    pool.sem_inc(pool_passed.sem, 1)
                    pool.tensor_tensor(to[2], nme[:], to[1], ALU.subtract).then_inc(nm_done.sem, 1)

            walk(pool, part)

        @block.scalar
        def _(sc):
            sc.wait_ge(loaded.sem, 16 * len(LOADS))

            def part(name, arg, i):
                if name == "ln_b":
                    sc.wait_ge(xt_done[arg].sem, xt_done[arg].of(i))
                    if arg in FFN:
                        sc.activation(hT[:], bt[:], ACT.Copy).then_inc(ht_done[arg].sem, 1)
                    else:
                        to, c = (hqT, 0) if arg == "attn" else (hT, 2)
                        if arg == "attn":
                            sc.wait_ge(x_full.sem, x_full.of(i - 1, X_FIRST["qkv", 1] + 2))
                        sc.activation(to[:], bt[:], ACT.Identity, bias=cols[:, c + 1:c + 2],
                                      scale=cols[:, c:c + 1]).then_inc(ht_done[arg].sem, 1)
                elif name == "gate":
                    b, c = arg
                    sc.wait_ge(gate_done[b].sem, gate_done[b].of(i, c + 1))
                    sc.wait_ge(sg_done[b].sem, sg_done[b].of(i, c))
                    sc.activation(th[:], bg[:], ACT.Tanh, scale=0.5).then_inc(tanh_done[b].sem, 1)
                elif name == "oT":
                    sc.wait_ge(ot_tr.sem, ot_tr.of(i))
                    sc.activation(oT[:], bt[:], ACT.Copy).then_inc(ot_done.sem, 1)
                elif name == "gelu":
                    for c in range(CF):
                        sc.wait_ge(w1_done.sem, w1_done.of(i, c + 1))
                        sc.activation(act[:, c], (bg, bu)[c % 2][:], ACT.Gelu, bias=cols[:, 4 + c:5 + c])\
                            .then_inc(gelu_done.sem, 1)
                elif name == "split":
                    s = arg
                    sc.wait_ge(r_done.sem, r_done.of(i, 2 * s + 2))
                    sc.wait_ge(stack_done.sem, stack_done.of(i, s))
                    sc.activation(part1[:], r[:], ACT.Copy).then_inc(p1_done.sem, 1)
                    sc.wait_ge(e1_done.sem, e1_done.of(i, s + 1))
                    sc.activation(part2[:], e1[:], ACT.Copy).then_inc(p2_done.sem, 1)
                elif name == "main":
                    g = arg
                    sc.wait_ge(pv_done.sem, pv_done.of(i, g - 1))
                    for b in range(3):
                        n = 3 * g + b
                        sc.wait_ge(m_full.sem, m_full.of(i, n + 1))
                        sc.activation(pT[:, g % 2, b], bm[n % 2][:], ACT.Exp, scale=HD ** -0.5)\
                            .then_inc(m_free.sem, 1)
                elif name == "pv":
                    sc.wait_ge(pv_done.sem, pv_done.of(i, arg + 1))
                    sc.activation(oq[:], bo[:, 0:T], ACT.Copy).then_inc(oq_done.sem, 1)

            walk(sc, part)

        @block.tensor
        def _(pe):
            pe.wait_ge(loaded.sem, 16 * len(LOADS))
            pe.wait_ge(consts_done.sem, 7)
            pe.wait_ge(stacks_set.sem, 3)

            def take_x(i, n):
                pe.wait_ge(x_free.sem, x_free.of(i, n - 1))
                return bx[n % 2]

            def part(name, arg, i):
                if name == "ln_b":
                    pe.wait_ge(xn_done[arg].sem, xn_done[arg].of(i))
                    for t in range(NT):
                        mm = pe.transpose(bt[:, t * P:(t + 1) * P], xn[:, t], ident[:])
                    mm.then_inc(xt_done[arg].sem, 1)
                elif name == "gate":
                    b, c = arg
                    pe.wait_ge(ht_done[b].sem, ht_done[b].of(i))
                    pe.wait_ge(mul_done[b].sem, mul_done[b].of(i, c))
                    pe.matmul(bg[:], wgate[:, c * P:(c + 1) * P], hT[:], start=True, stop=True).then_inc(gate_done[b].sem, 1)
                    pe.matmul(bu[:], wup[:, c * P:(c + 1) * P], hT[:], start=True, stop=True).then_inc(up_done[b].sem, 1)
                elif name == "down":
                    pe.wait_ge(mul_done[arg].sem, mul_done[arg].of(i))
                    for t in range(NT):
                        for c in range(CH):
                            mm = pe.matmul(bt[:, t * D:(t + 1) * D], act[:, c, t * P:(t + 1) * P], wdown[:, c],
                                           start=(c == 0), stop=(c == CH - 1))
                    mm.then_inc(down_done[arg].sem, 1)
                elif name == "oT":
                    pe.wait_ge(on_done.sem, on_done.of(i))
                    for t in range(NT):
                        mm = pe.transpose(bt[:, t * P:(t + 1) * P], on[:, t], ident[:])
                    mm.then_inc(ot_tr.sem, 1)
                elif name == "wo":
                    pe.wait_ge(ot_done.sem, ot_done.of(i))
                    for t in range(NT):
                        mm = pe.matmul(bt[:, t * D:(t + 1) * D], oT[:, t * P:(t + 1) * P], wo[:], start=True, stop=True)
                    mm.then_inc(wo_done.sem, 1)
                elif name == "w1":
                    pe.wait_ge(ht_done["gelu"].sem, ht_done["gelu"].of(i))
                    for c in (arg, arg + 1):
                        if c >= 2:
                            pe.wait_ge(gelu_done.sem, gelu_done.of(i, c - 1))
                        pe.matmul((bg, bu)[c % 2][:], w1[:, c * P:(c + 1) * P], hT[:], start=True, stop=True)\
                            .then_inc(w1_done.sem, 1)
                elif name == "w2":
                    pe.wait_ge(gelu_done.sem, gelu_done.of(i))
                    for t in range(NT):
                        for c in range(CF):
                            mm = pe.matmul(bt[:, t * D:(t + 1) * D], act[:, c, t * P:(t + 1) * P], w2[:, c],
                                           start=(c == 0), stop=(c == CF - 1))
                    mm.then_inc(w2_done.sem, 1)
                elif name == "qkv":
                    if arg == 0:
                        pe.wait_ge(ht_done["attn"].sem, ht_done["attn"].of(i))
                    for t in range(2):
                        n = X_FIRST["qkv", arg] + t
                        at = (2 * arg + t) * P
                        pe.matmul(take_x(i, n)[:, 0:3 * D], hqT[:, at:at + P], wqkv[:], start=True, stop=True)\
                            .then_inc(x_full.sem, 1)
                elif name == "stackT":
                    s = arg
                    pe.wait_ge(stack_done.sem, stack_done.of(i, s + 1))
                    pe.wait_ge(nm_clear.sem, nm_clear.of(i, s + 1))
                    for b in range(4):
                        n = X_FIRST["stackT", s] + b
                        to = take_x(i, n)[:].bitcast(BF16)
                        src = (ks, qs)[b % 2]
                        for h2 in range(4):
                            for t in range(2):
                                at = t * H + 8 * (b // 2) + 2 * h2
                                mm = pe.transpose(to[:, h2 * T + t * P:h2 * T + (t + 1) * P],
                                                  src[:, s, at:at + 2].rearrange("p h c -> p (h c)"), identb[:])
                        mm.then_inc(x_full.sem, 1)
                elif name == "max":
                    s, heads, rows_h = heads_of(arg)
                    heads = range(H)[heads]
                    if arg % 4 == 0:
                        pe.wait_ge(x_free.sem, x_free.of(i, X_FIRST["stackT", s] + 4))
                    for b in range(3):
                        to = take_x(i, X_FIRST["max", arg] + b)
                        tile = min(b, 1)
                        w = P if tile == 0 else T
                        pe.matmul(to[:], identb[:], mask_max[:, tile], start=True, stop=False, skip_group_check=True)
                        for c, h in enumerate(heads if tile == 0 else heads[2 * (b - 1):2 * b]):
                            mm = pe.matmul(to[:, c * w:(c + 1) * w], qT[rows_h, s, h // 2, tile * P:(tile + 1) * P],
                                           kT[rows_h, s, h // 2, 0:w], start=False, stop=True, skip_group_check=True)
                        mm.then_inc(x_full.sem, 1)
                elif name == "q2T":
                    o, s = arg, arg // 2
                    pe.wait_ge(nm_done.sem, nm_done.of(i, 4 * o + 4))
                    to = take_x(i, X_FIRST["q2T", o])[:].bitcast(BF16)
                    for h2 in range(4):
                        for t in range(2):
                            at = t * H + 8 * (o % 2) + 2 * h2
                            mm = pe.transpose(to[:, h2 * T + t * P:h2 * T + (t + 1) * P],
                                              qs[:, s, at:at + 2].rearrange("p h c -> p (h c)"), identb[:])
                    mm.then_inc(x_full.sem, 1)
                elif name == "main":
                    g = arg
                    s, heads, rows_h = heads_of(g)
                    heads = range(H)[heads]
                    pe.wait_ge(x_free.sem, x_free.of(i, X_FIRST["q2T", g // 2] + 1))
                    for b in range(3):
                        n = 3 * g + b
                        pe.wait_ge(m_free.sem, m_free.of(i, n - 1))
                        to = bm[n % 2]
                        tile = b // 2
                        w = T if tile == 0 else P
                        pe.matmul(to[:], identb[:], mask_main[:, tile], start=True, stop=False, skip_group_check=True)
                        for c, h in enumerate(heads if tile == 1 else heads[2 * b:2 * b + 2]):
                            mm = pe.matmul(to[:, c * w:(c + 1) * w], kT[rows_h, s, h // 2, tile * P:(tile + 1) * P],
                                           q2T[rows_h, g // 2 % 2, h % 8 // 2, T - w:T], start=False, stop=True,
                                           skip_group_check=True)
                        mm.then_inc(m_full.sem, 1)
                elif name == "pv":
                    g = arg
                    s, heads, _ = heads_of(g)
                    pe.wait_ge(m_free.sem, m_free.of(i, 3 * g + 3))
                    pe.wait_ge(on_done.sem, on_done.of(i, g))
                    for c, h in enumerate(range(H)[heads]):
                        pe.matmul(bo[32 * c:32 * c + 32, 0:T], vs[:, s, h],
                                  pT[:, g % 2, c // 2, (c % 2) * T:(c % 2 + 1) * T], start=True, stop=False, skip_group_check=True)
                    for c, h in enumerate(range(H)[heads]):
                        mm = pe.matmul(bo[32 * c:32 * c + 32, P:T], vs[:, s, H + h],
                                       pT[:, g % 2, 2, c * P:(c + 1) * P], start=False, stop=True, skip_group_check=True)
                    mm.then_inc(pv_done.sem, 1)
                elif name == "norm":
                    pe.wait_ge(oq_done.sem, oq_done.of(i, arg + 1))
                    for t in range(2):
                        mm = pe.transpose(bo[:, T + t * P:T + (t + 1) * P], oq[:, t * P:(t + 1) * P], ident[:])
                    mm.then_inc(oqt_done.sem, 1)

            walk(pe, part)

        @block.vector
        def _(ve):
            ve.wait_ge(loaded.sem, 16 * len(LOADS))
            ve.tensor_scalar(wgate[:], gate_i[:], SCALE, None, ALU.mult).then_inc(consts_done.sem, 1)
            ve.tensor_scalar(wup[:], up_i[:], SCALE, 0.5, ALU.mult, ALU.mult).then_inc(consts_done.sem, 1)
            ve.tensor_scalar(wdown[:].rearrange("p c d -> p (c d)"), down_i[:], SCALE, 0.5, ALU.mult, ALU.mult)\
                .then_inc(consts_done.sem, 1)
            ve.tensor_tensor(wo[:], wo[:], rows[:, 0], ALU.mult).then_inc(consts_done.sem, 1)
            for c in range(CF):
                ins = ve.tensor_tensor(w2[:, c], w2[:, c], rows[:, 1], ALU.mult)
            ins.then_inc(consts_done.sem, 1)
            ve.tensor_tensor(b2l[:], rows[:, 2], rows[:, 1], ALU.mult).then_inc(consts_done.sem, 2)
            ve.wait_ge(stacks_set.sem, 3)

            def part(name, arg, i):
                if name == "ln_a":
                    src, ready = {"ffn1": (x_in, x_loaded), "attn": (x1, x1_done),
                                  "gelu": (u2, u2_done), "ffn2": (x2, x2_done)}[arg]
                    ve.wait_ge(ready.sem, ready.of(i))
                    for t in range(NT):
                        ins = ve.bn_stats(stats[:, t], src[:, t])
                    ins.then_inc(bn_done[arg].sem, 1)
                    if arg == "ffn1":
                        ve.wait_ge(u_done.sem, u_done.of(i - 1))
                    ve.wait_ge(bn_done[arg].sem, bn_done[arg].of(i))
                    ve.sem_inc(vector_passed.sem, 1)
                    for t in range(NT):
                        ins = ve.bn_aggr(mv[:, t], stats[:, t])
                    ins.then_inc(mv_done[arg].sem, 1)
                elif name == "ln_b":
                    src = {"ffn1": x_in, "attn": x1, "gelu": u2, "ffn2": x2}[arg]
                    ve.wait_ge(rs_done[arg].sem, rs_done[arg].of(i))
                    r0 = rstd[:, 0]
                    if arg == "attn":
                        ve.tensor_tensor(lnr[:], rstd[:, 0], rstd[:, 1], ALU.mult).then_inc(lnr_done.sem, 1)
                        ve.wait_ge(lnr_done.sem, lnr_done.of(i))
                        r0 = lnr
                    for t in range(NT):
                        ins = ve.tensor_scalar(xn[:, t], src[:, t], mv[:, t, 0:1], r0[:, t:t + 1], ALU.subtract, ALU.mult)
                    ins.then_inc(xn_done[arg].sem, 1)
                elif name == "gate":
                    b, c = arg
                    ve.wait_ge(tanh_done[b].sem, tanh_done[b].of(i, c + 1))
                    ve.scalar_tensor_tensor(sg[:], th[:], 1.0, bg[:], ALU.add, ALU.mult).then_inc(sg_done[b].sem, 1)
                    ve.wait_ge(sg_done[b].sem, sg_done[b].of(i, c + 1))
                    ve.wait_ge(up_done[b].sem, up_done[b].of(i, c + 1))
                    ve.tensor_tensor(act[:, c], sg[:], bu[:], ALU.mult).then_inc(mul_done[b].sem, 1)
                elif name == "down":
                    ve.wait_ge(down_done[arg].sem, down_done[arg].of(i))
                    y = bt[:].rearrange("p (t d) -> p t d", t=NT)
                    if arg == "ffn1":
                        ve.wait_ge(u_done.sem, u_done.of(i - 1))
                        ve.tensor_tensor(x1[:], x_in[:], y, ALU.add).then_inc(x1_done.sem, 1)
                    else:
                        ve.wait_ge(out_stored.sem, out_stored.of(i - 1))
                        ve.tensor_tensor(xout[:], x2[:], y, ALU.add).then_inc(out_done.sem, 1)
                elif name == "wo":
                    ve.wait_ge(wo_done.sem, wo_done.of(i))
                    ve.wait_ge(handed.sem, handed.of(i))
                    ve.wait_ge(ux_done.sem, ux_done.of(i - 1))
                    ve.tensor_tensor(u2[:], u_back[:], bt[:].rearrange("p (t d) -> p t d", t=NT), ALU.add)\
                        .then_inc(u2_done.sem, 1)
                elif name == "w2":
                    ve.wait_ge(w2_done.sem, w2_done.of(i))
                    ve.wait_ge(ux_done.sem, ux_done.of(i))
                    ve.tensor_tensor(x2[:], ux[:], bt[:].rearrange("p (t d) -> p t d", t=NT), ALU.add)\
                        .then_inc(x2_done.sem, 1)
                elif name == "qkv":
                    for t in range(2):
                        n = X_FIRST["qkv", arg] + t
                        ve.wait_ge(x_full.sem, x_full.of(i, n + 1))
                        ve.wait_ge(r_done.sem, r_done.of(i, 2 * arg + t - 1))
                        src = bx[n % 2]
                        ve.tensor_tensor(rot1[:, t], src[:, 0:2 * D], cosr[:, t], ALU.mult)
                        for half in range(2):
                            def cut(ap, k):
                                return ap.rearrange("p (h c) -> p h c", c=HD)[:, :, HD // 2 * k:HD // 2 * (k + 1)]
                            ins = ve.tensor_tensor(cut(rot2[:, t], half), cut(src[:, 0:2 * D], 1 - half),
                                                   cut(sinr[:, t], half), ALU.mult)
                        ins.then_inc(rot_done.sem, 1)
                        if t == 0:
                            ve.wait_ge(pv_done.sem, pv_done.of(i - 1, 4 * arg + 4))
                        ve.tensor_copy(vs[:, arg, t * H:(t + 1) * H, 0:HD],
                                       src[:, 2 * D:3 * D].rearrange("p (h c) -> p h c", c=HD)).then_inc(x_free.sem, 1)
                elif name == "split":
                    s = arg
                    ve.wait_ge(p3_done.sem, p3_done.of(i, s + 1))
                    ve.wait_ge(x_full.sem, x_full.of(i - 1, X_FIRST["q2T", 2 * s + 1] + 1))
                    q1, q2, q3 = (z[:, 0].rearrange("p (h c) -> p h c", c=HD) for z in (part1, part2, part3))
                    k1, k2, k3 = (z[:, 1].rearrange("p (h c) -> p h c", c=HD) for z in (part1, part2, part3))
                    for c, z in ((0, q1), (8, q1), (16, q1), (24, q3), (40, q2), (48, q2)):
                        ve.tensor_copy(qs[:, s, :, c:c + HD], z)
                    for c, z in ((0, k1), (8, k2), (16, k3), (24, k1), (40, k1), (48, k2)):
                        ins = ve.tensor_copy(ks[:, s, :, c:c + HD], z)
                    ins.then_inc(stack_done.sem, 1)
                elif name == "stackT":
                    s = arg
                    ve.wait_ge(m_full.sem, m_full.of(i - 1, 3 * (4 * s + 3) + 3))
                    for b in range(4):
                        n = X_FIRST["stackT", s] + b
                        ve.wait_ge(x_full.sem, x_full.of(i, n + 1))
                        to = (kT, qT)[b % 2]
                        ve.tensor_copy(to[:, s, 4 * (b // 2):4 * (b // 2) + 4],
                                       bx[n % 2][:].bitcast(BF16).rearrange("p (h t) -> p h t", h=4)).then_inc(x_free.sem, 1)
                elif name == "max":
                    s, heads, _ = heads_of(arg)
                    ve.wait_ge(nm_done.sem, nm_done.of(i - 1, 4 * (arg // 2) + 4))
                    for b in range(3):
                        n = X_FIRST["max", arg] + b
                        ve.wait_ge(x_full.sem, x_full.of(i, n + 1))
                        tile = min(b, 1)
                        to = nmax[:, s, tile, heads]
                        if tile == 1:
                            to = to[:, 2 * (b - 1):2 * b]
                        ve.tensor_reduce(to, bx[n % 2][:].rearrange("p (h c) -> p h c", h=4 if tile == 0 else 2),
                                         AX.X, ALU.max, negate=True).then_inc(x_free.sem, 1)
                elif name == "q2T":
                    o = arg
                    n = X_FIRST["q2T", o]
                    ve.wait_ge(x_full.sem, x_full.of(i, n + 1))
                    ve.wait_ge(m_full.sem, m_full.of(i, 6 * (o - 1)))
                    ve.tensor_copy(q2T[:, o % 2], bx[n % 2][:].bitcast(BF16).rearrange("p (h t) -> p h t", h=4))\
                        .then_inc(x_free.sem, 1)
                elif name == "norm":
                    g = arg
                    s, heads, _ = heads_of(g)
                    ve.wait_ge(oqt_done.sem, oqt_done.of(i, g + 1))
                    y = bo[:, T:2 * T].rearrange("p (h c) -> p h c", c=32)
                    ve.reciprocal(rden[:], y[:, :, HD]).then_inc(rden_done.sem, 1)
                    ve.wait_ge(rden_done.sem, rden_done.of(i, g + 1))
                    ve.wait_ge(ot_tr.sem, ot_tr.of(i - 1))
                    ve.tensor_tensor(on[:, 2 * s:2 * s + 2].rearrange("p t (h c) -> p t h c", c=HD)[:, :, heads],
                                     bo[:, T:2 * T].rearrange("p (t h c) -> p t h c", t=2, c=32)[:, :, :, 0:HD],
                                     rden[:].rearrange("p (t h) -> p t h", t=2).unsqueeze(3).to_broadcast([P, 2, QUAD, HD]),
                                     ALU.mult).then_inc(on_done.sem, 1)

            walk(ve, part)


_OUT = (B, T, D)


def constants():
    f = np.float32
    inv = (f(1.0) / np.power(f(10000.0), np.arange(0, HD, 2, dtype=f) / f(HD))).astype(f)
    ang = np.outer(np.arange(T, dtype=f), inv).astype(f)
    cos, sin = np.cos(ang).astype(f), np.sin(ang).astype(f)
    cos = np.tile(np.concatenate([cos, cos], 1), (1, 2 * H)).reshape(2, P, 2 * D).transpose(1, 0, 2)
    sin = np.tile(np.concatenate([-sin, sin], 1), (1, 2 * H)).reshape(2, P, 2 * D).transpose(1, 0, 2)
    t, s = np.arange(T)[:, None], np.arange(T)[None, :]
    ok = (t >= s) & (t - s < WINDOW)
    m = np.where(ok, f(0), f(MASKED))
    bf = mybir.dt.np(BF16)
    mask_max = np.stack([np.tile(m[:P, :P], (1, 4)), np.tile(m[P:], (1, 2))], 1).astype(bf)
    mask_main = np.stack([np.tile(m.T[:P], (1, 2)), np.tile(m.T[P:, P:], (1, 4))], 1).astype(bf)
    return {"cos": cos, "sin": sin, "ident": np.eye(P, dtype=f), "identb": np.eye(P).astype(bf),
            "mask_max": mask_max, "mask_main": mask_main}


def kernel(**inputs):
    import concourse.bacc as _bacc
    from concourse.bass_utils import run_bass_kernel_spmd as _run

    z = {k.removeprefix("L0_attn_").removeprefix("L0_ffn_"): np.asarray(v) for k, v in inputs.items()}
    arrays = constants()
    arrays["x"] = z["x"].reshape(B * T, D)
    arrays["wqkv"] = np.concatenate([z["wq"].T, z["wk"].T, z["wv"].T], 1)
    arrays["wo"] = z["wo"].T
    arrays["w1"] = z["w1"].T
    arrays["w2"] = z["w2"].T.reshape(CF, P, D).transpose(1, 0, 2)
    arrays["w_gate"] = z["w_gate"].T
    arrays["w_up"] = z["w_up"].T
    arrays["w_down"] = z["w_down"].T.reshape(CH, P, D).transpose(1, 0, 2).reshape(P, CH * D)
    arrays["cols"] = np.concatenate([z[n].reshape(P, 1) for n in ("norm1_w", "norm1_b", "norm2_w", "norm2_b")]
                                    + [z["b1"].reshape(CF, P).T], 1)
    arrays["rows"] = np.broadcast_to(np.stack([z["ls1"], z["ls2"], z["b2"]])[None], (P, 3, D))
    nc = _bacc.Bacc("TRN2", target_bir_lowering=False, num_devices=1)
    arrays = {f"in_{k}": np.ascontiguousarray(v) for k, v in arrays.items()}
    aps = {k[3:]: nc.dram_tensor(k, v.shape, mybir.dt.from_np(v.dtype), kind="ExternalInput").ap() for k, v in arrays.items()}
    aps["out"] = nc.dram_tensor("out_y", (B * T, D), F32, kind="ExternalOutput").ap()
    build(nc, aps)
    res = _run(nc, [arrays], core_ids=[0])
    return res.results[0]["out_y"].reshape(_OUT)
```

```python
from contextlib import ExitStack

import numpy as np
import concourse.bass as bass
from concourse import mybir
from concourse.alu_op_type import AluOpType as ALU

ACT = mybir.ActivationFunctionType
AX = mybir.AxisListType
F32 = mybir.dt.float32
BF16 = mybir.dt.bfloat16
I32 = mybir.dt.int32

P = 128
B, T, D = 32, 256, 128
H, HD = 16, 8
FF, HID = 512, 384
WINDOW = 125
EPS = 1e-5
SCALE = float(np.float32(1.0 / 127.0))
NT = 4
PAIRS = B * T // (NT * P)
TOK = NT * P
QUAD = 4
GROUPS = 2 * H // QUAD
CH, CF = HID // P, FF // P

STK = 64
MCOL = 32
MASKED = -1e30

PE_ORDER = (
    ("qkv", 0, 0), ("oT",), ("qkv", 0, 1), ("wo",), ("lnT", "gelu"), ("stk", 0, 0), ("stk", 0, 1), ("stk", 0, 2),
    ("max", 0, 0), ("w1", 0), ("stk", 0, 3), ("qkv", 1, 0), ("qkv", 1, 1), ("w1", 1), ("max", 0, 1), ("max", 0, 2),
    ("w1", 2), ("max", 1, 0), ("max", 1, 1), ("w1", 3), ("max", 1, 2), ("max", 2, 0), ("max", 2, 1), ("w2",),
    ("q2T", 0), ("max", 2, 2), ("stk", 1, 0), ("main", 0, 0), ("stk", 1, 1), ("main", 0, 1), ("lnT", "ffn2"),
    ("max", 3, 0), ("max", 3, 1), ("gate", "ffn2", 0), ("max", 3, 2), ("main", 0, 2), ("max", 4, 0), ("main", 1, 0),
    ("max", 4, 1), ("pv", 0), ("gate", "ffn2", 1), ("stk", 1, 2), ("q2T", 1), ("main", 1, 1), ("gate", "ffn2", 2),
    ("max", 4, 2), ("max", 5, 0), ("main", 1, 2), ("oqT", 0), ("main", 2, 0), ("max", 5, 1), ("main", 2, 1),
    ("down", "ffn2"), ("stk", 1, 3), ("pv", 1), ("max", 5, 2), ("main", 2, 2), ("main", 3, 0), ("max", 6, 0),
    ("oqT", 1), ("main", 3, 1), ("main", 3, 2), ("lnT", "ffn1"), ("q2T", 2), ("max", 6, 1), ("gate", "ffn1", 0),
    ("pv", 2), ("max", 6, 2), ("main", 4, 0), ("oqT", 2), ("max", 7, 0), ("gate", "ffn1", 1), ("max", 7, 1),
    ("main", 4, 1), ("pv", 3), ("max", 7, 2), ("main", 4, 2), ("gate", "ffn1", 2), ("oqT", 3), ("main", 5, 0),
    ("pv", 4), ("q2T", 3), ("down", "ffn1"), ("main", 5, 1), ("main", 5, 2), ("oqT", 4), ("main", 6, 0),
    ("main", 6, 1), ("pv", 5), ("main", 6, 2), ("oqT", 5), ("main", 7, 0), ("main", 7, 1), ("pv", 6), ("main", 7, 2),
    ("oqT", 6), ("lnT", "attn"), ("pv", 7), ("oqT", 7),
)
VE_ORDER = (
    ("rot", 0, 0), ("rot", 0, 1), ("u2",), ("stat", "gelu"), ("lnx", "gelu"), ("stack", 0), ("stkx", 0, 0),
    ("stkx", 0, 1), ("stkx", 0, 2), ("mx", 0, 0), ("stkx", 0, 3), ("rot", 1, 0), ("rot", 1, 1), ("mx", 0, 1),
    ("mx", 0, 2), ("mx", 1, 0), ("mx", 1, 1), ("mx", 1, 2), ("mx", 2, 0), ("mx", 2, 1), ("stack", 1), ("x2",),
    ("stat", "ffn2"), ("q2x", 0), ("mx", 2, 2), ("lnx", "ffn2"), ("stkx", 1, 0), ("stkx", 1, 1), ("mx", 3, 0),
    ("mx", 3, 1), ("mx", 3, 2), ("silu", "ffn2", 0), ("mx", 4, 0), ("mx", 4, 1), ("silu", "ffn2", 1), ("stkx", 1, 2),
    ("q2x", 1), ("mx", 4, 2), ("silu", "ffn2", 2), ("mx", 5, 0), ("norm", 0), ("mx", 5, 1), ("res", "ffn2"),
    ("stat", "ffn1"), ("stkx", 1, 3), ("mx", 5, 2), ("lnx", "ffn1"), ("mx", 6, 0), ("norm", 1), ("q2x", 2),
    ("mx", 6, 1), ("silu", "ffn1", 0), ("mx", 6, 2), ("norm", 2), ("mx", 7, 0), ("silu", "ffn1", 1), ("mx", 7, 1),
    ("mx", 7, 2), ("norm", 3), ("silu", "ffn1", 2), ("q2x", 3), ("res", "ffn1"), ("stat", "attn"), ("norm", 4),
    ("norm", 5), ("lnx", "attn"), ("norm", 6), ("norm", 7),
)
SC_ORDER = (
    ("oTx",), ("p1", 0), ("p2", 0), ("lnh", "gelu"), ("gelu", 0), ("gelu", 1), ("p1", 1), ("gelu", 2), ("p2", 1),
    ("gelu", 3), ("lnh", "ffn2"), ("exp", 0, 0), ("exp", 0, 1), ("tanh", "ffn2", 0), ("exp", 0, 2), ("exp", 1, 0),
    ("oq", 0), ("tanh", "ffn2", 1), ("tanh", "ffn2", 2), ("exp", 1, 1), ("exp", 1, 2), ("exp", 2, 0), ("hand",),
    ("exp", 2, 1), ("oq", 1), ("exp", 2, 2), ("exp", 3, 0), ("exp", 3, 1), ("lnh", "ffn1"), ("tanh", "ffn1", 0),
    ("oq", 2), ("exp", 3, 2), ("tanh", "ffn1", 1), ("exp", 4, 0), ("oq", 3), ("exp", 4, 1), ("exp", 4, 2),
    ("tanh", "ffn1", 2), ("exp", 5, 0), ("oq", 4), ("exp", 5, 1), ("exp", 5, 2), ("exp", 6, 0), ("exp", 6, 1),
    ("oq", 5), ("exp", 6, 2), ("exp", 7, 0), ("exp", 7, 1), ("oq", 6), ("exp", 7, 2), ("lnh", "attn"), ("oq", 7),
)
POOL_ORDER = (
    ("add", 0, 0), ("add", 0, 1), ("e1", 0), ("rs", "gelu"), ("e3", 0), ("add", 1, 0), ("add", 1, 1), ("e1", 1),
    ("ux",), ("e3", 1), ("nm", 0), ("rs", "ffn2"), ("nm", 1), ("rs", "ffn1"), ("nm", 2), ("nm", 3), ("rs", "attn"),
    ("uu", "attn"),
)


ATTN = {"qkv", "stk", "max", "q2T", "main", "pv", "oqT", "rot", "stack", "stkx", "mx", "q2x", "norm", "p1", "p2", "exp", "oq",
        "add", "e1", "e3", "nm", "hand"}
BACK = {"oT", "wo", "w1", "w2", "oTx", "gelu", "u2", "x2", "ux"}


def stage_of(name, *which):
    if name in ATTN:
        return 0
    return -1 if name in BACK or which[0] in ("gelu", "ffn2") else 1


X_AT = {_part: _n for _n, _part in enumerate(p for p in PE_ORDER if p[0] in ("qkv", "stk", "max", "q2T"))}
X_USES = len(X_AT)
assert X_USES % 2 == 0


def x_last(name, whiches):
    return 1 + max(X_AT[(name, *w)] for w in whiches)


def heads_of(g):
    s, j = g // 4, g % 4
    first = 8 * (j // 2) + j % 2
    return s, slice(first, first + 7, 2), slice(STK * (j % 2), STK * (j % 2) + STK)


class Count:

    def __init__(self, sem, per):
        self.sem, self.per = sem, per

    def of(self, pair, n=None):
        value = pair * self.per + (self.per if n is None else n)
        return max(value, 0) if isinstance(value, int) else value


def build(nc, a):
    with ExitStack() as ctx:
        def sb(name, shape, dt=F32):
            return ctx.enter_context(nc.sbuf_tensor(name, shape, dt))

        def bank(name):
            return ctx.enter_context(nc.psum_tensor(name, [P, 512], F32))

        def count(name, per=1):
            return Count(ctx.enter_context(nc.semaphore(name)), per)

        ident = sb("ident", [P, P])
        identb = sb("identb", [P, P], BF16)
        mask_max = sb("mask_max", [P, 2, T])
        mask_main = sb("mask_main", [P, 2, 512], BF16)
        cosr = sb("cosr", [P, 2, 2 * D])
        sinr = sb("sinr", [P, 2, 2 * D])
        wqkv = sb("wqkv", [P, 3 * D])
        wo = sb("wo", [P, D])
        w1 = sb("w1", [P, FF])
        w2 = sb("w2", [P, CF, D])
        gate_i = sb("gate_i", [P, HID], I32)
        up_i = sb("up_i", [P, HID], I32)
        down_i = sb("down_i", [P, CH * D], I32)
        wgate = sb("wgate", [P, HID])
        wup = sb("wup", [P, HID])
        wdown = sb("wdown", [P, CH, D])
        cols = sb("cols", [P, 4 + CF])
        rows = sb("rows", [P, 3, D])
        b2l = sb("b2l", [P, D])
        mhalf = sb("mhalf", [P, NT])

        x_in = sb("x_in", [P, NT, D])
        x1 = sb("x1", [P, NT, D])
        u = sb("u", [P, NT, D])
        x1b = sb("x1b", [P, NT, D])
        u_back = sb("u_back", [P, NT, D])
        x1b_back = sb("x1b_back", [P, NT, D])
        u2 = sb("u2", [P, NT, D])
        ux = sb("ux", [P, NT, D])
        x2 = sb("x2", [P, NT, D])
        xout = sb("xout", [P, NT, D])
        stats = sb("stats", [P, NT, 6])
        LN = ("ffn1", "attn", "gelu", "ffn2")
        mv = {b: sb(f"mv_{b}", [P, NT, 2]) for b in LN}
        lnv = sb("lnv", [P, 4, NT])
        rstd = {b: sb(f"rstd_{b}", [P, NT]) for b in LN}
        rstd_u = sb("rstd_u", [P, NT])
        lnr = sb("lnr", [P, NT])
        xn = sb("xn", [P, NT, D])
        hT = sb("hT", [P, TOK])
        hqT = sb("hqT", [P, TOK])
        th = sb("th", [P, TOK])
        sg = sb("sg", [P, TOK])
        act = sb("act", [P, CF, TOK])

        rot1 = sb("rot1", [P, 2, 2 * D])
        rot2 = sb("rot2", [P, 2, 2 * D])
        r = sb("r", [P, 2, 2 * D])
        e1 = sb("e1", [P, 2, 2 * D])
        part1 = sb("part1", [P, 2, 2 * D], BF16)
        part2 = sb("part2", [P, 2, 2 * D], BF16)
        part3 = sb("part3", [P, 2, 2 * D], BF16)
        qs = sb("qs", [P, 2, 2 * H, STK], BF16)
        ks = sb("ks", [P, 2, 2 * H, STK], BF16)
        vs = sb("vs", [P, 2, 2 * H, 32])
        qT = sb("qT", [P, 2, H // 2, T], BF16)
        kT = sb("kT", [P, 2, H // 2, T], BF16)
        q2T = sb("q2T", [P, 2, 4, T], BF16)
        nmax = sb("nmax", [P, 2, 2, H])
        nme = sb("nme", [P, 2, 8])
        masked = sb("masked", [P, 2, 512], BF16)
        pT = sb("pT", [P, 2, 3, 512])
        oq = sb("oq", [P, T])
        rden = sb("rden", [P, 2 * QUAD])
        on = sb("on", [P, NT, D])
        oT = sb("oT", [P, TOK])

        bx = [bank("bx0"), bank("bx1")]
        bm = [bank("bm0"), bank("bm1")]
        bo = bank("bo")
        bt = bank("bt")
        bg, bu = bank("bg"), bank("bu")

        loaded = count("loaded")
        consts_done = count("consts_done")
        stacks_set = count("stacks_set")
        x_loaded = count("x_loaded", 16)
        out_stored = count("out_stored", 16)
        bn_done = {b: count(f"bn_{b}") for b in LN}
        mv_done = {b: count(f"mv_{b}") for b in LN}
        rs_done = {b: count(f"rs_{b}", 6 if b == "attn" else 2) for b in LN}
        xn_done = {b: count(f"xn_{b}") for b in LN}
        xt_done = {b: count(f"xt_{b}") for b in LN}
        ht_done = {b: count(f"ht_{b}") for b in LN}
        FFN = ("ffn1", "ffn2")
        gate_done = {b: count(f"gate_{b}", CH) for b in FFN}
        up_done = {b: count(f"up_{b}", CH) for b in FFN}
        tanh_done = {b: count(f"tanh_{b}", CH) for b in FFN}
        sg_done = {b: count(f"sg_{b}", CH) for b in FFN}
        mul_done = {b: count(f"mul_{b}", CH) for b in FFN}
        down_done = {b: count(f"down_{b}") for b in FFN}
        lnr_done = count("lnr_done")
        x1_done = count("x1_done")
        u_done = count("u_done")
        handed = count("handed")
        ot_tr = count("ot_tr")
        ot_done = count("ot_done")
        wo_done = count("wo_done")
        u2_done = count("u2_done")
        ux_done = count("ux_done")
        w1_done = count("w1_done", CF)
        gelu_done = count("gelu_done", CF)
        w2_done = count("w2_done")
        x2_done = count("x2_done")
        out_done = count("out_done")
        x_full = count("x_full", X_USES)
        x_free = count("x_free", X_USES)
        rot_done = count("rot_done", NT)
        r_done = count("r_done", NT)
        p1_done = count("p1_done", 2)
        e1_done = count("e1_done", 2)
        p2_done = count("p2_done", 2)
        p3_done = count("p3_done", 2)
        stack_done = count("stack_done", 2)
        nm_clear = count("nm_clear", 2)
        nm_done = count("nm_done", 4 * GROUPS // 2)
        m_full = count("m_full", 3 * GROUPS)
        m_free = count("m_free", 3 * GROUPS)
        pv_done = count("pv_done", GROUPS)
        oq_done = count("oq_done", GROUPS)
        oqt_done = count("oqt_done", GROUPS)
        rden_done = count("rden_done", GROUPS)
        on_done = count("on_done", GROUPS)

        pool_passed = count("pool_passed")
        vector_passed = count("vector_passed")

        def walk(eng, order, part):
            def step(k, stages):
                for name, *which in order:
                    stage = stage_of(name, *which)
                    if stage in stages:
                        part(k + stage, name, *which)
            step(-1, (1,))
            step(0, (0, 1))
            with eng.Fori(1, PAIRS - 1) as k:
                step(k, (0, -1, 1))
            step(PAIRS - 1, (0, -1))
            step(PAIRS, (-1,))

        block = ctx.enter_context(nc.Block())

        x_view = a["x"].rearrange("(i t p) d -> i p t d", t=NT, p=P)
        out_view = a["out"].rearrange("(i t p) d -> i p t d", t=NT, p=P)
        LOADS = [(ident, "ident"), (identb, "identb"), (gate_i, "w_gate"), (up_i, "w_up"), (down_i, "w_down"),
                 (cols, "cols"), (rows, "rows"), (wqkv, "wqkv"), (cosr, "cos"), (sinr, "sin"),
                 (mask_max, "mask_max"), (mask_main, "mask_main"), (wo, "wo"), (w1, "w1"), (w2, "w2")]

        @block.sync
        def _(sp):
            def load_x(i):
                sp.wait_ge(x1_done.sem, x1_done.of(i - 1))
                sp.dma_start(x_in[:], x_view[i]).then_inc(x_loaded.sem, 16)

            def store(i):
                sp.wait_ge(out_done.sem, out_done.of(i))
                sp.dma_start(out_view[i], xout[:]).then_inc(out_stored.sem, 16)

            load_x(0)
            for tile, name in LOADS:
                sp.dma_start(tile[:], a[name]).then_inc(loaded.sem, 16)
            load_x(1)
            with sp.Fori(1, PAIRS - 1) as k:
                load_x(k + 1)
                store(k - 1)
            store(PAIRS - 2)
            store(PAIRS - 1)
            sp.wait_ge(out_stored.sem, 16 * PAIRS)

        @block.gpsimd
        def _(pool):
            pool.memset(mhalf[:], -0.5)
            pool.memset(qs[:], 0.0)
            pool.memset(ks[:], 0.0)
            pool.memset(vs[:], 0.0).then_inc(stacks_set.sem, 1)
            pool.wait_ge(stacks_set.sem, 1)
            for s in range(2):
                pool.memset(ks[:, s, :, MCOL:MCOL + 3], 1.0)
                pool.memset(vs[:, s, :, HD:HD + 1], 1.0).then_inc(stacks_set.sem, 1)
            pool.wait_ge(consts_done.sem, 7)

            def part(i, name, w=None, t=None):
                if name == "rs":
                    rs = rs_done[w]
                    pool.wait_ge(mv_done[w].sem, mv_done[w].of(i))
                    pool.sem_inc(pool_passed.sem, 1)
                    pool.tensor_scalar(lnv[:, 0], mv[w][:, :, 1], EPS, None, ALU.add).then_inc(rs.sem, 1)
                    pool.wait_ge(rs.sem, rs.of(i, 1))
                    if w != "attn":
                        pool.tensor_tensor(rstd[w][:], lnv[:, 0], mhalf[:], ALU.pow).then_inc(rs.sem, 1)
                        return
                    pool.tensor_tensor(rstd_u[:], lnv[:, 0], mhalf[:], ALU.pow).then_inc(rs.sem, 1)
                    pool.wait_ge(rs.sem, rs.of(i, 2))
                    pool.tensor_tensor(lnv[:, 1], mv[w][:, :, 1], rstd_u[:], ALU.mult).then_inc(rs.sem, 1)
                    pool.wait_ge(rs.sem, rs.of(i, 3))
                    pool.tensor_tensor(lnv[:, 2], lnv[:, 1], rstd_u[:], ALU.mult).then_inc(rs.sem, 1)
                    pool.wait_ge(rs.sem, rs.of(i, 4))
                    pool.sem_inc(pool_passed.sem, 1)
                    pool.tensor_scalar(lnv[:, 3], lnv[:, 2], EPS, None, ALU.add).then_inc(rs.sem, 1)
                    pool.wait_ge(rs.sem, rs.of(i, 5))
                    pool.tensor_tensor(rstd[w][:], lnv[:, 3], mhalf[:], ALU.pow).then_inc(rs.sem, 1)
                elif name == "uu":
                    pool.wait_ge(handed.sem, handed.of(i - 1))
                    pool.tensor_tensor(x1b[:, 0], x1[:, 0], b2l[:], ALU.add)
                    for n in range(1, NT):
                        pool.tensor_tensor(x1b[:, n], x1[:, n], b2l[:], ALU.add)
                    for n in range(NT):
                        ins = pool.tensor_scalar(u[:, n], x1[:, n], mv["attn"][:, n, 0:1], rstd_u[:, n:n + 1],
                                                 ALU.subtract, ALU.mult)
                    ins.then_inc(u_done.sem, 1)
                elif name == "ux":
                    pool.wait_ge(handed.sem, handed.of(i))
                    pool.wait_ge(u2_done.sem, u2_done.of(i))
                    pool.wait_ge(x2_done.sem, x2_done.of(i - 1))
                    pool.tensor_tensor(ux[:], u2[:], x1b_back[:], ALU.add).then_inc(ux_done.sem, 1)
                elif name == "add":
                    pool.wait_ge(rot_done.sem, rot_done.of(i, 2 * w + t + 1))
                    if t == 0:
                        pool.wait_ge(p3_done.sem, p3_done.of(i, w))
                    pool.tensor_tensor(r[:, :, t * D:(t + 1) * D],
                                       rot1[:, t].rearrange("p (a c) -> p a c", a=2),
                                       rot2[:, t].rearrange("p (a c) -> p a c", a=2), ALU.add).then_inc(r_done.sem, 1)
                elif name == "e1":
                    pool.wait_ge(p1_done.sem, p1_done.of(i, w + 1))
                    pool.tensor_tensor(e1[:], r[:], part1[:], ALU.subtract).then_inc(e1_done.sem, 1)
                elif name == "e3":
                    pool.wait_ge(stack_done.sem, stack_done.of(i, w))
                    pool.wait_ge(p2_done.sem, p2_done.of(i, w + 1))
                    pool.tensor_tensor(part3[:], e1[:], part2[:], ALU.subtract).then_inc(p3_done.sem, 1)
                    pool.wait_ge(x_full.sem, x_full.of(i - 1, x_last("q2T", ((2 * w,), (2 * w + 1,)))))
                    pool.sem_inc(pool_passed.sem, 1)
                    pool.memset(qs[:, w, :, MCOL:MCOL + 3], 0.0).then_inc(nm_clear.sem, 1)
                elif name == "nm":
                    o, s = w, w // 2
                    pool.wait_ge(x_free.sem, x_free.of(i, x_last("max", [(g, b) for g in (2 * o, 2 * o + 1) for b in range(3)])))
                    pool.wait_ge(x_full.sem, x_full.of(i, x_last("stk", [(s, b) for b in range(4)])))
                    pool.sem_inc(pool_passed.sem, 1)
                    hs = slice(8 * (o % 2), 8 * (o % 2) + 8)
                    nm = nmax[:, s, :, hs]
                    to = [qs[:, s, :, MCOL + c].rearrange("p (t h) -> p t h", t=2)[:, :, hs] for c in range(3)]
                    pool.tensor_copy(to[0], nm).then_inc(nm_done.sem, 1)
                    pool.wait_ge(nm_done.sem, nm_done.of(i, 4 * o + 1))
                    pool.tensor_tensor(nme[:], nm, to[0], ALU.subtract).then_inc(nm_done.sem, 1)
                    pool.wait_ge(nm_done.sem, nm_done.of(i, 4 * o + 2))
                    pool.sem_inc(pool_passed.sem, 1)
                    pool.tensor_copy(to[1], nme[:]).then_inc(nm_done.sem, 1)
                    pool.wait_ge(nm_done.sem, nm_done.of(i, 4 * o + 3))
                    pool.tensor_tensor(to[2], nme[:], to[1], ALU.subtract).then_inc(nm_done.sem, 1)

            walk(pool, POOL_ORDER, part)

        @block.scalar
        def _(sc):
            sc.wait_ge(loaded.sem, 16 * len(LOADS))

            def part(i, name, w=None, c=None):
                if name == "lnh":
                    sc.wait_ge(xt_done[w].sem, xt_done[w].of(i))
                    if w in FFN:
                        sc.activation(hT[:], bt[:], ACT.Copy).then_inc(ht_done[w].sem, 1)
                        return
                    to, at = (hqT, 0) if w == "attn" else (hT, 2)
                    if w == "attn":
                        sc.wait_ge(x_full.sem, x_full.of(i - 1, x_last("qkv", [(1, 1)])))
                    sc.activation(to[:], bt[:], ACT.Identity, bias=cols[:, at + 1:at + 2],
                                  scale=cols[:, at:at + 1]).then_inc(ht_done[w].sem, 1)
                elif name == "tanh":
                    sc.wait_ge(sg_done[w].sem, sg_done[w].of(i, c))
                    sc.wait_ge(gate_done[w].sem, gate_done[w].of(i, c + 1))
                    sc.activation(th[:], bg[:], ACT.Tanh, scale=0.5).then_inc(tanh_done[w].sem, 1)
                elif name == "oTx":
                    sc.wait_ge(ot_tr.sem, ot_tr.of(i))
                    sc.activation(oT[:], bt[:], ACT.Copy).then_inc(ot_done.sem, 1)
                elif name == "gelu":
                    sc.wait_ge(w1_done.sem, w1_done.of(i, w + 1))
                    sc.activation(act[:, w], (bg, bu)[w % 2][:], ACT.Gelu, bias=cols[:, 4 + w:5 + w]).then_inc(gelu_done.sem, 1)
                elif name == "p1":
                    sc.wait_ge(stack_done.sem, stack_done.of(i, w))
                    sc.wait_ge(r_done.sem, r_done.of(i, 2 * w + 2))
                    sc.activation(part1[:], r[:], ACT.Copy).then_inc(p1_done.sem, 1)
                elif name == "p2":
                    sc.wait_ge(e1_done.sem, e1_done.of(i, w + 1))
                    sc.activation(part2[:], e1[:], ACT.Copy).then_inc(p2_done.sem, 1)
                elif name == "exp":
                    n = 3 * w + c
                    sc.wait_ge(pv_done.sem, pv_done.of(i, w - 1))
                    sc.wait_ge(m_full.sem, m_full.of(i, n + 1))
                    sc.activation(pT[:, w % 2, c], bm[n % 2][:], ACT.Exp, scale=HD ** -0.5).then_inc(m_free.sem, 1)
                elif name == "oq":
                    sc.wait_ge(pv_done.sem, pv_done.of(i, w + 1))
                    sc.activation(oq[:], bo[:, 0:T], ACT.Copy).then_inc(oq_done.sem, 1)
                elif name == "hand":
                    sc.wait_ge(u_done.sem, u_done.of(i))
                    sc.wait_ge(u2_done.sem, u2_done.of(i - 1))
                    sc.wait_ge(ux_done.sem, ux_done.of(i - 1))
                    sc.activation(u_back[:], u[:], ACT.Copy)
                    sc.activation(x1b_back[:], x1b[:], ACT.Copy).then_inc(handed.sem, 1)

            walk(sc, SC_ORDER, part)

        @block.tensor
        def _(pe):
            pe.wait_ge(loaded.sem, 16 * len(LOADS))
            pe.wait_ge(consts_done.sem, 7)
            pe.wait_ge(stacks_set.sem, 3)

            def take_x(i, n):
                pe.wait_ge(x_free.sem, x_free.of(i, n - 1))
                return bx[n % 2]

            def part(i, name, w=None, c=None):
                if name == "lnT":
                    pe.wait_ge(xn_done[w].sem, xn_done[w].of(i))
                    for t in range(NT):
                        mm = pe.transpose(bt[:, t * P:(t + 1) * P], xn[:, t], ident[:])
                    mm.then_inc(xt_done[w].sem, 1)
                elif name == "gate":
                    pe.wait_ge(ht_done[w].sem, ht_done[w].of(i))
                    pe.wait_ge(mul_done[w].sem, mul_done[w].of(i, c))
                    pe.matmul(bg[:], wgate[:, c * P:(c + 1) * P], hT[:], start=True, stop=True).then_inc(gate_done[w].sem, 1)
                    pe.matmul(bu[:], wup[:, c * P:(c + 1) * P], hT[:], start=True, stop=True).then_inc(up_done[w].sem, 1)
                elif name == "down":
                    pe.wait_ge(mul_done[w].sem, mul_done[w].of(i))
                    for t in range(NT):
                        for n in range(CH):
                            mm = pe.matmul(bt[:, t * D:(t + 1) * D], act[:, n, t * P:(t + 1) * P], wdown[:, n],
                                           start=(n == 0), stop=(n == CH - 1))
                    mm.then_inc(down_done[w].sem, 1)
                elif name == "oT":
                    pe.wait_ge(on_done.sem, on_done.of(i))
                    for t in range(NT):
                        mm = pe.transpose(bt[:, t * P:(t + 1) * P], on[:, t], ident[:])
                    mm.then_inc(ot_tr.sem, 1)
                elif name == "wo":
                    pe.wait_ge(ot_done.sem, ot_done.of(i))
                    for t in range(NT):
                        mm = pe.matmul(bt[:, t * D:(t + 1) * D], oT[:, t * P:(t + 1) * P], wo[:], start=True, stop=True)
                    mm.then_inc(wo_done.sem, 1)
                elif name == "w1":
                    pe.wait_ge(ht_done["gelu"].sem, ht_done["gelu"].of(i))
                    if w >= 2:
                        pe.wait_ge(gelu_done.sem, gelu_done.of(i, w - 1))
                    pe.matmul((bg, bu)[w % 2][:], w1[:, w * P:(w + 1) * P], hT[:], start=True, stop=True)\
                        .then_inc(w1_done.sem, 1)
                elif name == "w2":
                    pe.wait_ge(gelu_done.sem, gelu_done.of(i))
                    for t in range(NT):
                        for n in range(CF):
                            mm = pe.matmul(bt[:, t * D:(t + 1) * D], act[:, n, t * P:(t + 1) * P], w2[:, n],
                                           start=(n == 0), stop=(n == CF - 1))
                    mm.then_inc(w2_done.sem, 1)
                elif name == "qkv":
                    pe.wait_ge(ht_done["attn"].sem, ht_done["attn"].of(i))
                    at = (2 * w + c) * P
                    pe.matmul(take_x(i, X_AT["qkv", w, c])[:, 0:3 * D], hqT[:, at:at + P], wqkv[:], start=True, stop=True)\
                        .then_inc(x_full.sem, 1)
                elif name == "stk":
                    pe.wait_ge(stack_done.sem, stack_done.of(i, w + 1))
                    pe.wait_ge(nm_clear.sem, nm_clear.of(i, w + 1))
                    to = take_x(i, X_AT["stk", w, c])[:].bitcast(BF16)
                    src = (ks, qs)[c % 2]
                    for h2 in range(4):
                        for t in range(2):
                            at = t * H + 8 * (c // 2) + 2 * h2
                            mm = pe.transpose(to[:, h2 * T + t * P:h2 * T + (t + 1) * P],
                                              src[:, w, at:at + 2].rearrange("p h c -> p (h c)"), identb[:])
                    mm.then_inc(x_full.sem, 1)
                elif name == "max":
                    s, heads, rows_h = heads_of(w)
                    heads = range(H)[heads]
                    pe.wait_ge(x_free.sem, x_free.of(i, x_last("stk", [(s, 2 * (w % 4 // 2) + n) for n in range(2)])))
                    to = take_x(i, X_AT["max", w, c])
                    tile = min(c, 1)
                    n = P if tile == 0 else T
                    for at, h in enumerate(heads if tile == 0 else heads[2 * (c - 1):2 * c]):
                        mm = pe.matmul(to[:, at * n:(at + 1) * n], qT[rows_h, s, h // 2, tile * P:(tile + 1) * P],
                                       kT[rows_h, s, h // 2, 0:n], start=True, stop=True)
                    mm.then_inc(x_full.sem, 1)
                elif name == "q2T":
                    s = w // 2
                    pe.wait_ge(nm_done.sem, nm_done.of(i, 4 * w + 4))
                    to = take_x(i, X_AT["q2T", w])[:].bitcast(BF16)
                    for h2 in range(4):
                        for t in range(2):
                            at = t * H + 8 * (w % 2) + 2 * h2
                            mm = pe.transpose(to[:, h2 * T + t * P:h2 * T + (t + 1) * P],
                                              qs[:, s, at:at + 2].rearrange("p h c -> p (h c)"), identb[:])
                    mm.then_inc(x_full.sem, 1)
                elif name == "main":
                    s, heads, rows_h = heads_of(w)
                    heads = range(H)[heads]
                    pe.wait_ge(x_free.sem, x_free.of(i, x_last("q2T", [(w // 2,)])))
                    n = 3 * w + c
                    if n >= 2:
                        pe.wait_ge(m_free.sem, m_free.of(i, n - 1))
                    else:
                        pe.wait_ge(m_free.sem, m_free.of(i - 1, m_free.per + n - 1))
                    to = bm[n % 2]
                    tile = c // 2
                    n = T if tile == 0 else P
                    pe.matmul(to[:], identb[:], mask_main[:, tile], start=True, stop=False, skip_group_check=True)
                    for at, h in enumerate(heads if tile == 1 else heads[2 * c:2 * c + 2]):
                        mm = pe.matmul(to[:, at * n:(at + 1) * n], kT[rows_h, s, h // 2, tile * P:(tile + 1) * P],
                                       q2T[rows_h, w // 2 % 2, h % 8 // 2, T - n:T], start=False, stop=True,
                                       skip_group_check=True)
                    mm.then_inc(m_full.sem, 1)
                elif name == "pv":
                    s, heads, _ = heads_of(w)
                    pe.wait_ge(m_free.sem, m_free.of(i, 3 * w + 3))
                    pe.wait_ge(on_done.sem, on_done.of(i, w))
                    for n, h in enumerate(range(H)[heads]):
                        pe.matmul(bo[32 * n:32 * n + 32, 0:T], vs[:, s, h],
                                  pT[:, w % 2, n // 2, (n % 2) * T:(n % 2 + 1) * T], start=True, stop=False, skip_group_check=True)
                    for n, h in enumerate(range(H)[heads]):
                        mm = pe.matmul(bo[32 * n:32 * n + 32, P:T], vs[:, s, H + h],
                                       pT[:, w % 2, 2, n * P:(n + 1) * P], start=False, stop=True, skip_group_check=True)
                    mm.then_inc(pv_done.sem, 1)
                elif name == "oqT":
                    pe.wait_ge(oq_done.sem, oq_done.of(i, w + 1))
                    for t in range(2):
                        mm = pe.transpose(bo[:, T + t * P:T + (t + 1) * P], oq[:, t * P:(t + 1) * P], ident[:])
                    mm.then_inc(oqt_done.sem, 1)

            walk(pe, PE_ORDER, part)

        @block.vector
        def _(ve):
            ve.wait_ge(loaded.sem, 16 * len(LOADS))
            ve.tensor_scalar(wgate[:], gate_i[:], SCALE, None, ALU.mult).then_inc(consts_done.sem, 1)
            ve.tensor_scalar(wup[:], up_i[:], SCALE, 0.5, ALU.mult, ALU.mult).then_inc(consts_done.sem, 1)
            ve.tensor_scalar(wdown[:].rearrange("p c d -> p (c d)"), down_i[:], SCALE, 0.5, ALU.mult, ALU.mult)\
                .then_inc(consts_done.sem, 1)
            ve.tensor_tensor(wo[:], wo[:], rows[:, 0], ALU.mult).then_inc(consts_done.sem, 1)
            for c in range(CF):
                ins = ve.tensor_tensor(w2[:, c], w2[:, c], rows[:, 1], ALU.mult)
            ins.then_inc(consts_done.sem, 1)
            ve.tensor_tensor(b2l[:], rows[:, 2], rows[:, 1], ALU.mult).then_inc(consts_done.sem, 2)
            ve.wait_ge(stacks_set.sem, 3)

            def part(i, name, w=None, c=None):
                if name == "stat":
                    src, ready = {"ffn1": (x_in, x_loaded), "attn": (x1, x1_done),
                                  "gelu": (u2, u2_done), "ffn2": (x2, x2_done)}[w]
                    ve.wait_ge(ready.sem, ready.of(i))
                    for t in range(NT):
                        ins = ve.bn_stats(stats[:, t], src[:, t])
                    ins.then_inc(bn_done[w].sem, 1)
                    if w == "attn":
                        ve.wait_ge(u_done.sem, u_done.of(i - 1))
                    ve.wait_ge(bn_done[w].sem, bn_done[w].of(i))
                    ve.sem_inc(vector_passed.sem, 1)
                    for t in range(NT):
                        ins = ve.bn_aggr(mv[w][:, t], stats[:, t])
                    ins.then_inc(mv_done[w].sem, 1)
                elif name == "lnx":
                    src = {"ffn1": x_in, "attn": x1, "gelu": u2, "ffn2": x2}[w]
                    ve.wait_ge(rs_done[w].sem, rs_done[w].of(i))
                    by = rstd[w]
                    if w == "attn":
                        ve.tensor_tensor(lnr[:], rstd[w][:], rstd_u[:], ALU.mult).then_inc(lnr_done.sem, 1)
                        ve.wait_ge(lnr_done.sem, lnr_done.of(i))
                        by = lnr
                    for t in range(NT):
                        ins = ve.tensor_scalar(xn[:, t], src[:, t], mv[w][:, t, 0:1], by[:, t:t + 1], ALU.subtract, ALU.mult)
                    ins.then_inc(xn_done[w].sem, 1)
                elif name == "silu":
                    ve.wait_ge(tanh_done[w].sem, tanh_done[w].of(i, c + 1))
                    ve.scalar_tensor_tensor(sg[:], th[:], 1.0, bg[:], ALU.add, ALU.mult).then_inc(sg_done[w].sem, 1)
                    ve.wait_ge(sg_done[w].sem, sg_done[w].of(i, c + 1))
                    ve.wait_ge(up_done[w].sem, up_done[w].of(i, c + 1))
                    ve.tensor_tensor(act[:, c], sg[:], bu[:], ALU.mult).then_inc(mul_done[w].sem, 1)
                elif name == "res":
                    y = bt[:].rearrange("p (t d) -> p t d", t=NT)
                    if w == "ffn1":
                        ve.wait_ge(u_done.sem, u_done.of(i - 1))
                        ve.wait_ge(down_done[w].sem, down_done[w].of(i))
                        ve.tensor_tensor(x1[:], x_in[:], y, ALU.add).then_inc(x1_done.sem, 1)
                    else:
                        ve.wait_ge(out_stored.sem, out_stored.of(i - 1))
                        ve.wait_ge(down_done[w].sem, down_done[w].of(i))
                        ve.tensor_tensor(xout[:], x2[:], y, ALU.add).then_inc(out_done.sem, 1)
                elif name == "u2":
                    ve.wait_ge(handed.sem, handed.of(i))
                    ve.wait_ge(ux_done.sem, ux_done.of(i - 1))
                    ve.wait_ge(wo_done.sem, wo_done.of(i))
                    ve.tensor_tensor(u2[:], u_back[:], bt[:].rearrange("p (t d) -> p t d", t=NT), ALU.add)\
                        .then_inc(u2_done.sem, 1)
                elif name == "x2":
                    ve.wait_ge(ux_done.sem, ux_done.of(i))
                    ve.wait_ge(w2_done.sem, w2_done.of(i))
                    ve.tensor_tensor(x2[:], ux[:], bt[:].rearrange("p (t d) -> p t d", t=NT), ALU.add)\
                        .then_inc(x2_done.sem, 1)
                elif name == "rot":
                    n = X_AT["qkv", w, c]
                    if w == 1:
                        ve.wait_ge(r_done.sem, r_done.of(i, c + 1))
                    else:
                        ve.wait_ge(r_done.sem, r_done.of(i - 1, 3 + c))
                    ve.wait_ge(pv_done.sem, pv_done.of(i - 1, 4 * w + 4))
                    ve.wait_ge(x_full.sem, x_full.of(i, n + 1))
                    src = bx[n % 2]
                    ve.tensor_tensor(rot1[:, c], src[:, 0:2 * D], cosr[:, c], ALU.mult)
                    for half in range(2):
                        def cut(ap, k):
                            return ap.rearrange("p (h c) -> p h c", c=HD)[:, :, HD // 2 * k:HD // 2 * (k + 1)]
                        ins = ve.tensor_tensor(cut(rot2[:, c], half), cut(src[:, 0:2 * D], 1 - half),
                                               cut(sinr[:, c], half), ALU.mult)
                    ins.then_inc(rot_done.sem, 1)
                    ve.tensor_copy(vs[:, w, c * H:(c + 1) * H, 0:HD],
                                   src[:, 2 * D:3 * D].rearrange("p (h c) -> p h c", c=HD)).then_inc(x_free.sem, 1)
                elif name == "stack":
                    ve.wait_ge(p3_done.sem, p3_done.of(i, w + 1))
                    ve.wait_ge(x_full.sem, x_full.of(i - 1, x_last("q2T", ((2 * w,), (2 * w + 1,)))))
                    q1, q2, q3 = (z[:, 0].rearrange("p (h c) -> p h c", c=HD) for z in (part1, part2, part3))
                    k1, k2, k3 = (z[:, 1].rearrange("p (h c) -> p h c", c=HD) for z in (part1, part2, part3))
                    for at, z in ((0, q1), (8, q1), (16, q1), (24, q3), (40, q2), (48, q2)):
                        ve.tensor_copy(qs[:, w, :, at:at + HD], z)
                    for at, z in ((0, k1), (8, k2), (16, k3), (24, k1), (40, k1), (48, k2)):
                        ins = ve.tensor_copy(ks[:, w, :, at:at + HD], z)
                    ins.then_inc(stack_done.sem, 1)
                elif name == "stkx":
                    n = X_AT["stk", w, c]
                    ve.wait_ge(m_full.sem, m_full.of(i - 1, 12 * w + 12))
                    ve.wait_ge(x_full.sem, x_full.of(i, n + 1))
                    to = (kT, qT)[c % 2]
                    ve.tensor_copy(to[:, w, 4 * (c // 2):4 * (c // 2) + 4],
                                   bx[n % 2][:].bitcast(BF16).rearrange("p (h t) -> p h t", h=4)).then_inc(x_free.sem, 1)
                elif name == "mx":
                    s, heads, _ = heads_of(w)
                    heads = range(H)[heads]
                    n = X_AT["max", w, c]
                    ve.wait_ge(nm_done.sem, nm_done.of(i - 1, 4 * (w // 2) + 4))
                    ve.wait_ge(x_free.sem, x_free.of(i, n - 1))
                    ve.wait_ge(x_full.sem, x_full.of(i, n + 1))
                    ve.sem_inc(vector_passed.sem, 1)
                    tile = min(c, 1)
                    wide = P if tile == 0 else T
                    for at, h in enumerate(heads if tile == 0 else heads[2 * (c - 1):2 * c]):
                        ins = ve.tensor_tensor_reduce(masked[:, n % 2, at * wide:(at + 1) * wide], bx[n % 2][:, at * wide:(at + 1) * wide],
                                                      mask_max[:, tile, 0:wide], -1.0, -2 * MASKED, ALU.add, ALU.min,
                                                      nmax[:, s, tile, h:h + 1])
                    ins.then_inc(x_free.sem, 1)
                elif name == "q2x":
                    n = X_AT["q2T", w]
                    if w >= 2:
                        ve.wait_ge(m_full.sem, m_full.of(i, 6 * (w - 1)))
                    else:
                        ve.wait_ge(m_full.sem, m_full.of(i - 1, 6 * (w + 3)))
                    ve.wait_ge(x_full.sem, x_full.of(i, n + 1))
                    ve.tensor_copy(q2T[:, w % 2], bx[n % 2][:].bitcast(BF16).rearrange("p (h t) -> p h t", h=4))\
                        .then_inc(x_free.sem, 1)
                elif name == "norm":
                    s, heads, _ = heads_of(w)
                    ve.wait_ge(oqt_done.sem, oqt_done.of(i, w + 1))
                    y = bo[:, T:2 * T].rearrange("p (h c) -> p h c", c=32)
                    ve.reciprocal(rden[:], y[:, :, HD]).then_inc(rden_done.sem, 1)
                    ve.wait_ge(ot_tr.sem, ot_tr.of(i - 1))
                    ve.wait_ge(rden_done.sem, rden_done.of(i, w + 1))
                    ve.tensor_tensor(on[:, 2 * s:2 * s + 2].rearrange("p t (h c) -> p t h c", c=HD)[:, :, heads],
                                     bo[:, T:2 * T].rearrange("p (t h c) -> p t h c", t=2, c=32)[:, :, :, 0:HD],
                                     rden[:].rearrange("p (t h) -> p t h", t=2).unsqueeze(3).to_broadcast([P, 2, QUAD, HD]),
                                     ALU.mult).then_inc(on_done.sem, 1)

            walk(ve, VE_ORDER, part)


_OUT = (B, T, D)


def constants():
    f = np.float32
    inv = (f(1.0) / np.power(f(10000.0), np.arange(0, HD, 2, dtype=f) / f(HD))).astype(f)
    ang = np.outer(np.arange(T, dtype=f), inv).astype(f)
    cos, sin = np.cos(ang).astype(f), np.sin(ang).astype(f)
    cos = np.tile(np.concatenate([cos, cos], 1), (1, 2 * H)).reshape(2, P, 2 * D).transpose(1, 0, 2)
    sin = np.tile(np.concatenate([-sin, sin], 1), (1, 2 * H)).reshape(2, P, 2 * D).transpose(1, 0, 2)
    t, s = np.arange(T)[:, None], np.arange(T)[None, :]
    ok = (t >= s) & (t - s < WINDOW)
    m = np.where(ok, f(0), f(MASKED))
    bf = mybir.dt.np(BF16)
    mask_max = m.reshape(2, P, T).transpose(1, 0, 2)
    mask_main = np.stack([np.tile(m.T[:P], (1, 2)), np.tile(m.T[P:, P:], (1, 4))], 1).astype(bf)
    return {"cos": cos, "sin": sin, "ident": np.eye(P, dtype=f), "identb": np.eye(P).astype(bf),
            "mask_max": mask_max, "mask_main": mask_main}


def kernel(**inputs):
    import concourse.bacc as _bacc
    from concourse.bass_utils import run_bass_kernel_spmd as _run

    z = {k.removeprefix("L0_attn_").removeprefix("L0_ffn_"): np.asarray(v) for k, v in inputs.items()}
    arrays = constants()
    arrays["x"] = z["x"].reshape(B * T, D)
    arrays["wqkv"] = np.concatenate([z["wq"].T, z["wk"].T, z["wv"].T], 1)
    arrays["wo"] = z["wo"].T
    arrays["w1"] = z["w1"].T
    arrays["w2"] = z["w2"].T.reshape(CF, P, D).transpose(1, 0, 2)
    arrays["w_gate"] = z["w_gate"].T
    arrays["w_up"] = z["w_up"].T
    arrays["w_down"] = z["w_down"].T.reshape(CH, P, D).transpose(1, 0, 2).reshape(P, CH * D)
    arrays["cols"] = np.concatenate([z[n].reshape(P, 1) for n in ("norm1_w", "norm1_b", "norm2_w", "norm2_b")]
                                    + [z["b1"].reshape(CF, P).T], 1)
    arrays["rows"] = np.broadcast_to(np.stack([z["ls1"], z["ls2"], z["b2"]])[None], (P, 3, D))
    nc = _bacc.Bacc("TRN2", target_bir_lowering=False, num_devices=1)
    arrays = {f"in_{k}": np.ascontiguousarray(v) for k, v in arrays.items()}
    aps = {k[3:]: nc.dram_tensor(k, v.shape, mybir.dt.from_np(v.dtype), kind="ExternalInput").ap() for k, v in arrays.items()}
    aps["out"] = nc.dram_tensor("out_y", (B * T, D), F32, kind="ExternalOutput").ap()
    build(nc, aps)
    res = _run(nc, [arrays], core_ids=[0])
    return res.results[0]["out_y"].reshape(_OUT)
```

```python
from contextlib import ExitStack

import numpy as np
import concourse.bass as bass
from concourse import mybir
from concourse.alu_op_type import AluOpType as ALU

ACT = mybir.ActivationFunctionType
F32 = mybir.dt.float32
F32R = mybir.dt.float32r
BF16 = mybir.dt.bfloat16
I32 = mybir.dt.int32

P = 128
B, T, D = 32, 256, 128
H, HD = 16, 8
FF, HID = 512, 384
WINDOW = 125
EPS = 1e-5
SCALE = float(np.float32(1.0 / 127.0))
NT = 4
PAIRS = B * T // (NT * P)
TOK = NT * P
QUAD = 4
GROUPS = 2 * H // QUAD
CH, CF = HID // P, FF // P

STK = 64
MCOL = 32
MASKED = -1e30

PE_ORDER = (
    ("stk", 0, 1), ("oqT", 6), ("stk", 0, 2), ("max", 0, 0), ("pv", 7), ("max", 0, 1), ("oqT", 7), ("max", 0, 2),
    ("max", 1, 0), ("oT",), ("max", 1, 1), ("max", 1, 2), ("wo",), ("stk", 0, 3), ("qkv", 1, 0), ("q2T", 0),
    ("qkv", 1, 1), ("max", 2, 0), ("main", 0, 0), ("max", 2, 1), ("lnT", "gelu"), ("max", 2, 2), ("main", 0, 1),
    ("max", 3, 0), ("main", 0, 2), ("max", 3, 1), ("max", 3, 2), ("main", 1, 0), ("main", 1, 1), ("w1", 0), ("w1", 1),
    ("pv", 0), ("w1", 2), ("q2T", 1), ("w1", 3), ("lnT", "ffn1"), ("stk", 1, 0), ("oqT", 0), ("w2",), ("stk", 1, 1),
    ("gate", "ffn1", 0), ("up", "ffn1", 0), ("gate", "ffn1", 1), ("main", 1, 2), ("max", 4, 0), ("max", 4, 1),
    ("up", "ffn1", 1), ("main", 2, 0), ("gate", "ffn1", 2), ("up", "ffn1", 2), ("max", 4, 2), ("pv", 1),
    ("max", 5, 0), ("main", 2, 1), ("main", 2, 2), ("lnT", "ffn2"), ("max", 5, 1), ("oqT", 1), ("down", "ffn1"),
    ("stk", 1, 2), ("main", 3, 0), ("stk", 1, 3), ("pv", 2), ("max", 5, 2), ("main", 3, 1), ("max", 6, 0), ("oqT", 2),
    ("gate", "ffn2", 0), ("up", "ffn2", 0), ("gate", "ffn2", 1), ("max", 6, 1), ("max", 6, 2), ("main", 3, 2),
    ("up", "ffn2", 1), ("gate", "ffn2", 2), ("pv", 3), ("q2T", 2), ("lnT", "attn"), ("max", 7, 0), ("up", "ffn2", 2),
    ("main", 4, 0), ("max", 7, 1), ("main", 4, 1), ("max", 7, 2), ("oqT", 3), ("main", 4, 2), ("main", 5, 0),
    ("qkv", 0, 0), ("qkv", 0, 1), ("main", 5, 1), ("pv", 4), ("main", 5, 2), ("q2T", 3), ("oqT", 4), ("down", "ffn2"),
    ("pv", 5), ("main", 6, 0), ("main", 6, 1), ("oqT", 5), ("main", 6, 2), ("main", 7, 0), ("pv", 6), ("main", 7, 1),
    ("main", 7, 2), ("stk", 0, 0),
)
VE_ORDER = (
    ("stat", "ffn1"), ("norm", 5), ("stack", 0), ("stkx", 0, 0), ("norm", 6), ("stkx", 0, 2), ("mx", 0, 0),
    ("mx", 0, 1), ("norm", 7), ("mx", 0, 2), ("mx", 1, 0), ("mx", 1, 1), ("mx", 1, 2), ("u2",), ("stat", "gelu"),
    ("rot", 1, 0), ("q2x", 0), ("rot", 1, 1), ("mx", 2, 0), ("mx", 2, 1), ("mx", 2, 2), ("mx", 3, 0), ("mx", 3, 1),
    ("mx", 3, 2), ("stack", 1), ("q2x", 1), ("stkx", 1, 0), ("norm", 0), ("x2",), ("stat", "ffn2"), ("sg", "ffn1", 0),
    ("mul", "ffn1", 0), ("sg", "ffn1", 1), ("mx", 4, 0), ("mx", 4, 1), ("mul", "ffn1", 1), ("sg", "ffn1", 2),
    ("mx", 4, 2), ("mul", "ffn1", 2), ("mx", 5, 0), ("mx", 5, 1), ("norm", 1), ("res", "ffn1"), ("stkx", 1, 2),
    ("stat", "attn"), ("mx", 5, 2), ("mx", 6, 0), ("norm", 2), ("sg", "ffn2", 0), ("mul", "ffn2", 0),
    ("sg", "ffn2", 1), ("mx", 6, 1), ("mx", 6, 2), ("mul", "ffn2", 1), ("q2x", 2), ("mx", 7, 0), ("sg", "ffn2", 2),
    ("mx", 7, 1), ("mx", 7, 2), ("norm", 3), ("mul", "ffn2", 2), ("rot", 0, 0), ("rot", 0, 1), ("norm", 4),
    ("q2x", 3), ("res", "ffn2"),
)
SC_ORDER = (
    ("exp", 4, 0), ("exp", 4, 1), ("exp", 4, 2), ("exp", 5, 0), ("oq", 4), ("exp", 5, 1), ("exp", 5, 2), ("p1", 0),
    ("p2", 0), ("oq", 5), ("exp", 6, 0), ("exp", 6, 1), ("exp", 6, 2), ("exp", 7, 0), ("oq", 6), ("exp", 7, 1),
    ("exp", 7, 2), ("stkx", 0, 1), ("oq", 7), ("oTx",), ("lnx", "ffn1"), ("stkx", 0, 3), ("lnx", "gelu"),
    ("exp", 0, 0), ("p1", 1), ("lnh", "gelu"), ("exp", 0, 1), ("exp", 0, 2), ("p2", 1), ("gelu", 0), ("gelu", 1),
    ("gelu", 2), ("oq", 0), ("gelu", 3), ("hand",), ("lnh", "ffn1"), ("exp", 1, 0), ("stkx", 1, 1),
    ("tanh", "ffn1", 0), ("tanh", "ffn1", 1), ("exp", 1, 1), ("exp", 1, 2), ("exp", 2, 0), ("tanh", "ffn1", 2),
    ("lnx", "ffn2"), ("oq", 1), ("exp", 2, 1), ("exp", 2, 2), ("lnh", "ffn2"), ("stkx", 1, 3), ("oq", 2),
    ("exp", 3, 0), ("exp", 3, 1), ("tanh", "ffn2", 0), ("tanh", "ffn2", 1), ("exp", 3, 2), ("lnx", "attn"),
    ("tanh", "ffn2", 2), ("oq", 3), ("lnh", "attn"),
)
POOL_ORDER = (
    ("uu", "attn"), ("rs", "ffn1"), ("nm", 0), ("rs", "gelu"), ("add", 1, 0), ("add", 1, 1), ("ux",), ("e1", 1),
    ("lo", "gelu"), ("e3", 1), ("nm", 1), ("lo", "ffn1"), ("rs", "ffn2"), ("lo", "ffn2"), ("rs", "attn"), ("nm", 2),
    ("lo", "attn"), ("nm", 3), ("add", 0, 0), ("add", 0, 1), ("e1", 0), ("e3", 0),
)

EARLY = {
    ("stk", 0, 0),
}
LATE = {
    ("p1", 0), ("p2", 0), ("stack", 0), ("exp", 4, 0), ("exp", 4, 1), ("exp", 4, 2), ("oq", 4), ("exp", 5, 0),
    ("exp", 5, 1), ("exp", 5, 2), ("oq", 5), ("norm", 5), ("exp", 6, 0), ("exp", 6, 1), ("exp", 6, 2), ("oq", 6),
    ("oqT", 6), ("norm", 6), ("exp", 7, 0), ("exp", 7, 1), ("exp", 7, 2), ("pv", 7), ("oq", 7), ("oqT", 7),
    ("norm", 7), ("uu", "attn"),
}


ATTN = {"qkv", "stk", "max", "q2T", "main", "pv", "oqT", "rot", "stack", "stkx", "mx", "q2x", "norm", "p1", "p2", "exp", "oq",
        "add", "e1", "e3", "nm", "hand"}
PREPARE = {"qkv", "rot", "add", "p1", "e1", "p2", "e3", "stack"}
BACK = {"oT", "wo", "w1", "w2", "oTx", "gelu", "u2", "x2", "ux"}


def stage_of(*part):
    name, *which = part
    if name in PREPARE and which[0] == 0:
        stage = 1
    elif name in ATTN:
        stage = 0
    else:
        stage = -1 if name in BACK or which[0] in ("gelu", "ffn2") else 1
    return stage + (part in EARLY) - (part in LATE)


X_USES = [p for p in PE_ORDER if p[0] in ("qkv", "stk", "max", "q2T")]
D_USES = [p for p in PE_ORDER if p[0] in ("oT", "wo", "lnT", "w1", "w2", "gate", "up", "down")]
X_BANKS, D_BANKS = 2, 3
X_AT = {_part: _n % X_BANKS for _n, _part in enumerate(X_USES)}
D_AT = {_part: _n % D_BANKS for _n, _part in enumerate(D_USES)}


def before(k, part):
    uses, bank_of = (X_USES, X_AT) if part in X_AT else (D_USES, D_AT)
    at = uses.index(part)
    for back in range(3):
        for user in reversed(uses[:at] if back == 0 else uses):
            pair = k - back + stage_of(*user)
            if bank_of[user] == bank_of[part] and not (isinstance(k, int) and not 0 <= pair < PAIRS):
                return user, pair
    return None


def is_first(i):
    return isinstance(i, int) and i == 0


def heads_of(g):
    s, j = g // 4, g % 4
    first = 8 * (j // 2) + j % 2
    return s, slice(first, first + 7, 2), slice(STK * (j % 2), STK * (j % 2) + STK)


class Count:

    def __init__(self, sem, per):
        self.sem, self.per = sem, per

    def of(self, pair, n=None):
        value = pair * self.per + (self.per if n is None else n)
        return max(value, 0) if isinstance(value, int) else value


def build(nc, a):
    with ExitStack() as ctx:
        def sb(name, shape, dt=F32):
            return ctx.enter_context(nc.sbuf_tensor(name, shape, dt))

        def bank(name):
            return ctx.enter_context(nc.psum_tensor(name, [P, 512], F32))

        def count(name, per=1):
            return Count(ctx.enter_context(nc.semaphore(name)), per)

        ident = sb("ident", [P, P])
        identb = sb("identb", [P, P], BF16)
        mask_max = sb("mask_max", [P, 2, T])
        mask_main = sb("mask_main", [P, 2, 512], BF16)
        cosr = sb("cosr", [P, 2, 2 * D])
        sinr = sb("sinr", [P, 2, 2 * D])
        wqkv = sb("wqkv", [P, 3 * D])
        wo = sb("wo", [P, D])
        w1 = sb("w1", [P, FF])
        w2 = sb("w2", [P, CF, D])
        gate_i = sb("gate_i", [P, HID], I32)
        up_i = sb("up_i", [P, HID], I32)
        down_i = sb("down_i", [P, CH * D], I32)
        dequantised = sb("dequantised", [P, 2, HID])
        wdown = sb("wdown", [P, CH, D])
        cols = sb("cols", [P, 4 + CF])
        rows = sb("rows", [P, 3, D])
        b2l = sb("b2l", [P, D])
        mhalf = sb("mhalf", [P, NT])
        minus_one = sb("minus_one", [P, NT])
        wgate = [sb(f"wgate{n}", [P, HID], F32R) for n in range(2)]
        wup = [sb(f"wup{n}", [P, HID], F32R) for n in range(2)]
        wqkv2 = [sb(f"wqkv{n}", [P, 3 * D], F32R) for n in range(2)]
        w12 = [sb(f"w1{n}", [P, FF], F32R) for n in range(2)]

        x_in = sb("x_in", [P, NT, D])
        x1 = sb("x1", [P, NT, D])
        u = sb("u", [P, NT, D])
        x1b = sb("x1b", [P, NT, D])
        u_back = sb("u_back", [P, NT, D])
        x1b_back = sb("x1b_back", [P, NT, D])
        u2 = sb("u2", [P, NT, D])
        ux = sb("ux", [P, NT, D])
        x2 = sb("x2", [P, NT, D])
        xout = sb("xout", [P, NT, D])
        LN = ("ffn1", "attn", "gelu", "ffn2")
        stats = {b: sb(f"stats_{b}", [P, NT, 6]) for b in LN}
        mv = {b: sb(f"mv_{b}", [P, NT, 2]) for b in LN}
        lnv = {b: sb(f"lnv_{b}", [P, 4, NT]) for b in LN}
        rstd = {b: sb(f"rstd_{b}", [P, NT]) for b in LN}
        rstd_u = sb("rstd_u", [P, NT])
        lnr = sb("lnr", [P, NT])
        minus_mean = {b: sb(f"minus_mean_{b}", [P, NT]) for b in LN}
        shift = {b: sb(f"shift_{b}", [P, NT]) for b in LN}
        FRONT, BACK = 0, 1
        SIDE = {"ffn1": FRONT, "attn": FRONT, "gelu": BACK, "ffn2": BACK}
        xn = [sb(f"xn{n}", [P, NT, D]) for n in range(2)]
        full = {b: sb(f"full_{b}", [P, TOK]) for b in ("ffn1", "attn", "back")}
        hT = {b: [sb(f"hT_{b}{n}", [P, TOK], F32R) for n in range(2)] for b in ("ffn1", "attn", "back")}
        for b in ("gelu", "ffn2"):
            full[b], hT[b] = full["back"], hT["back"]
        th = [sb(f"th{n}", [P, 2, TOK]) for n in range(2)]
        sg = [sb(f"sg{n}", [P, 2, TOK]) for n in range(2)]
        act = [sb("act0", [P, CH, TOK]), sb("act1", [P, CF, TOK])]

        rot1 = sb("rot1", [P, 2, 2 * D])
        rot2 = sb("rot2", [P, 2, 2 * D])
        r = sb("r", [P, 2, 2 * D])
        e1 = sb("e1", [P, 2, 2 * D])
        part1 = sb("part1", [P, 2, 2 * D], BF16)
        part2 = sb("part2", [P, 2, 2 * D], BF16)
        part3 = sb("part3", [P, 2, 2 * D], BF16)
        qs = sb("qs", [P, 2, 2 * H, STK], BF16)
        ks = sb("ks", [P, 2, 2 * H, STK], BF16)
        vs = sb("vs", [P, 2, 2 * H, 32])
        qT = sb("qT", [P, 2, H // 2, T], BF16)
        kT = sb("kT", [P, 2, H // 2, T], BF16)
        q2T = sb("q2T", [P, 2, 4, T], BF16)
        nmax = sb("nmax", [P, 2, 2, H])
        nme = sb("nme", [P, 2, 8])
        masked = sb("masked", [P, 2, 512], BF16)
        pT = sb("pT", [P, 2, 3, 512])
        oq = sb("oq", [P, T])
        rden = sb("rden", [P, 2 * QUAD])
        on = sb("on", [P, NT, D])
        oT = sb("oT", [P, TOK])

        bx = [bank("bx0"), bank("bx1")]
        bm = [bank("bm0"), bank("bm1")]
        bo = bank("bo")
        bd = [bank(f"bd{n}") for n in range(D_BANKS)]

        ffn_loaded = count("ffn_loaded")
        loaded = count("loaded")
        dequant_done = count("dequant_done")
        split_done = count("split_done")
        scaled_done = count("scaled_done")
        stacks_set = count("stacks_set")
        x_loaded = count("x_loaded", 16)
        out_stored = count("out_stored", 16)
        bn_done = {b: count(f"bn_{b}") for b in LN}
        mv_done = {b: count(f"mv_{b}") for b in LN}
        rs_done = {b: count(f"rs_{b}", 8 if b == "attn" else 3) for b in LN}
        xn_done = {b: count(f"xn_{b}") for b in LN}
        xt_done = {b: count(f"xt_{b}") for b in LN}
        ht_done = {b: count(f"ht_{b}") for b in LN}
        lo_done = {b: count(f"lo_{b}") for b in LN}
        FFN = ("ffn1", "ffn2")
        gate_done = {b: count(f"gate_{b}", CH) for b in FFN}
        up_done = {b: count(f"up_{b}", CH) for b in FFN}
        tanh_done = {b: count(f"tanh_{b}", CH) for b in FFN}
        sg_done = {b: count(f"sg_{b}", CH) for b in FFN}
        mul_done = {b: count(f"mul_{b}", CH) for b in FFN}
        down_done = {b: count(f"down_{b}") for b in FFN}
        x1_done = count("x1_done")
        u_done = count("u_done")
        handed = count("handed")
        ot_tr = count("ot_tr")
        ot_done = count("ot_done")
        wo_done = count("wo_done")
        u2_done = count("u2_done")
        ux_done = count("ux_done")
        w1_done = count("w1_done", CF)
        gelu_done = count("gelu_done", CF)
        w2_done = count("w2_done")
        x2_done = count("x2_done")
        out_done = count("out_done")
        qkv_full = count("qkv_full", NT)
        vs_done = count("vs_done", NT)
        stk_full = count("stk_full", 8)
        kt_done = count("kt_done", 4)
        qt_done = count("qt_done", 4)
        max_full = count("max_full", 3 * GROUPS)
        mx_done = count("mx_done", 3 * GROUPS)
        q2t_full = count("q2t_full", 4)
        q2x_done = count("q2x_done", 4)
        rot_done = count("rot_done", NT)
        r_done = count("r_done", NT)
        p1_done = count("p1_done", 2)
        e1_done = count("e1_done", 2)
        p2_done = count("p2_done", 2)
        p3_done = count("p3_done", 2)
        stack_done = count("stack_done", 2)
        nm_clear = count("nm_clear", 2)
        nm_done = count("nm_done", 4 * GROUPS // 2)
        m_full = count("m_full", 3 * GROUPS)
        m_free = count("m_free", 3 * GROUPS)
        pv_done = count("pv_done", GROUPS)
        oq_done = count("oq_done", GROUPS)
        oqt_done = count("oqt_done", GROUPS)
        rden_done = count("rden_done", GROUPS)
        on_done = count("on_done", GROUPS)

        pool_passed = count("pool_passed")
        vector_passed = count("vector_passed")

        def walk(eng, order, part):
            def step(k):
                for name, *which in order:
                    i = k + stage_of(name, *which)
                    if not isinstance(k, int) or 0 <= i < PAIRS:
                        part(k, i, name, *which)

            for k in (-1, 0, 1):
                step(k)
            with eng.Fori(2, PAIRS - 1) as k:
                step(k)
            for k in (PAIRS - 1, PAIRS):
                step(k)

        block = ctx.enter_context(nc.Block())

        x_view = a["x"].rearrange("(i t p) d -> i p t d", t=NT, p=P)
        out_view = a["out"].rearrange("(i t p) d -> i p t d", t=NT, p=P)
        FFN_LOADS = [(gate_i, "w_gate"), (up_i, "w_up"), (ident, "ident")]
        LOADS = [(down_i, "w_down"), (wqkv, "wqkv"), (cols, "cols"), (rows, "rows"), (cosr, "cos"), (sinr, "sin"),
                 (identb, "identb"), (mask_max, "mask_max"), (mask_main, "mask_main"), (wo, "wo"), (w1, "w1"), (w2, "w2")]

        @block.sync
        def _(sp):
            def load_x(i):
                sp.wait_ge(x1_done.sem, x1_done.of(i - 1))
                sp.dma_start(x_in[:], x_view[i]).then_inc(x_loaded.sem, 16)

            def store(i):
                sp.wait_ge(out_done.sem, out_done.of(i))
                sp.dma_start(out_view[i], xout[:]).then_inc(out_stored.sem, 16)

            load_x(0)
            for tile, name in FFN_LOADS:
                sp.dma_start(tile[:], a[name]).then_inc(ffn_loaded.sem, 16)
            for tile, name in LOADS:
                sp.dma_start(tile[:], a[name]).then_inc(loaded.sem, 16)
            load_x(1)
            load_x(2)
            with sp.Fori(2, PAIRS - 1) as k:
                load_x(k + 1)
                store(k - 2)
            for i in range(PAIRS - 3, PAIRS):
                store(i)
            sp.wait_ge(out_stored.sem, 16 * PAIRS)

        @block.gpsimd
        def _(pool):
            pool.memset(mhalf[:], -0.5)
            pool.memset(minus_one[:], -1.0)
            pool.memset(ks[:], 0.0)
            pool.memset(vs[:], 0.0).then_inc(stacks_set.sem, 1)
            pool.wait_ge(stacks_set.sem, 2)
            for s in range(2):
                pool.memset(ks[:, s, :, MCOL:MCOL + 3], 1.0)
                pool.memset(vs[:, s, :, HD:HD + 1], 1.0).then_inc(stacks_set.sem, 1)

            def part(k, i, name, w=None, t=None):
                if name == "rs":
                    rs = rs_done[w]
                    pool.wait_ge(mv_done[w].sem, mv_done[w].of(i))
                    pool.sem_inc(pool_passed.sem, 1)
                    pool.tensor_tensor(minus_mean[w][:], mv[w][:, :, 0], minus_one[:], ALU.mult)
                    pool.tensor_scalar(lnv[w][:, 0], mv[w][:, :, 1], EPS, None, ALU.add).then_inc(rs.sem, 1)
                    pool.wait_ge(rs.sem, rs.of(i, 1))
                    if w != "attn":
                        pool.tensor_tensor(rstd[w][:], lnv[w][:, 0], mhalf[:], ALU.pow).then_inc(rs.sem, 1)
                        pool.wait_ge(rs.sem, rs.of(i, 2))
                        pool.tensor_tensor(shift[w][:], minus_mean[w][:], rstd[w][:], ALU.mult).then_inc(rs.sem, 1)
                        return
                    pool.tensor_tensor(rstd_u[:], lnv[w][:, 0], mhalf[:], ALU.pow).then_inc(rs.sem, 1)
                    pool.wait_ge(rs.sem, rs.of(i, 2))
                    pool.tensor_tensor(lnv[w][:, 1], mv[w][:, :, 1], rstd_u[:], ALU.mult).then_inc(rs.sem, 1)
                    pool.wait_ge(rs.sem, rs.of(i, 3))
                    pool.tensor_tensor(lnv[w][:, 2], lnv[w][:, 1], rstd_u[:], ALU.mult).then_inc(rs.sem, 1)
                    pool.wait_ge(rs.sem, rs.of(i, 4))
                    pool.sem_inc(pool_passed.sem, 1)
                    pool.tensor_scalar(lnv[w][:, 3], lnv[w][:, 2], EPS, None, ALU.add).then_inc(rs.sem, 1)
                    pool.wait_ge(rs.sem, rs.of(i, 5))
                    pool.tensor_tensor(rstd[w][:], lnv[w][:, 3], mhalf[:], ALU.pow).then_inc(rs.sem, 1)
                    pool.wait_ge(rs.sem, rs.of(i, 6))
                    pool.tensor_tensor(lnr[:], rstd[w][:], rstd_u[:], ALU.mult).then_inc(rs.sem, 1)
                    pool.wait_ge(rs.sem, rs.of(i, 7))
                    pool.tensor_tensor(shift[w][:], minus_mean[w][:], lnr[:], ALU.mult).then_inc(rs.sem, 1)
                elif name == "lo":
                    pool.wait_ge(ht_done[w].sem, ht_done[w].of(i))
                    pool.tensor_tensor(hT[w][1][:], full[w][:], hT[w][0][:].bitcast(F32), ALU.subtract).then_inc(lo_done[w].sem, 1)
                elif name == "uu":
                    pool.wait_ge(handed.sem, handed.of(i - 1))
                    if is_first(i):
                        pool.wait_ge(scaled_done.sem, 4)
                    pool.tensor_tensor(x1b[:, 0], x1[:, 0], b2l[:], ALU.add)
                    for n in range(1, NT):
                        pool.tensor_tensor(x1b[:, n], x1[:, n], b2l[:], ALU.add)
                    for n in range(NT):
                        ins = pool.tensor_scalar(u[:, n], x1[:, n], mv["attn"][:, n, 0:1], rstd_u[:, n:n + 1],
                                                 ALU.subtract, ALU.mult)
                    ins.then_inc(u_done.sem, 1)
                elif name == "ux":
                    pool.wait_ge(handed.sem, handed.of(i))
                    pool.wait_ge(u2_done.sem, u2_done.of(i))
                    pool.wait_ge(x2_done.sem, x2_done.of(i - 1))
                    pool.tensor_tensor(ux[:], u2[:], x1b_back[:], ALU.add).then_inc(ux_done.sem, 1)
                elif name == "add":
                    pool.wait_ge(rot_done.sem, rot_done.of(i, 2 * w + t + 1))
                    if t == 0:
                        pool.wait_ge(p3_done.sem, p3_done.of(i, w))
                    pool.tensor_tensor(r[:, :, t * D:(t + 1) * D],
                                       rot1[:, t].rearrange("p (a c) -> p a c", a=2),
                                       rot2[:, t].rearrange("p (a c) -> p a c", a=2), ALU.add).then_inc(r_done.sem, 1)
                elif name == "e1":
                    pool.wait_ge(p1_done.sem, p1_done.of(i, w + 1))
                    pool.tensor_tensor(e1[:], r[:], part1[:], ALU.subtract).then_inc(e1_done.sem, 1)
                elif name == "e3":
                    pool.wait_ge(stack_done.sem, stack_done.of(i, w))
                    pool.wait_ge(p2_done.sem, p2_done.of(i, w + 1))
                    pool.tensor_tensor(part3[:], e1[:], part2[:], ALU.subtract).then_inc(p3_done.sem, 1)
                    pool.wait_ge(q2t_full.sem, q2t_full.of(i - 1, 2 * w + 2))
                    pool.sem_inc(pool_passed.sem, 1)
                    pool.memset(qs[:, w, :, MCOL:MCOL + 3], 0.0).then_inc(nm_clear.sem, 1)
                elif name == "nm":
                    o, s = w, w // 2
                    pool.wait_ge(mx_done.sem, mx_done.of(i, 6 * o + 6))
                    pool.wait_ge(stk_full.sem, stk_full.of(i, 4 * s + 4))
                    pool.sem_inc(pool_passed.sem, 1)
                    hs = slice(8 * (o % 2), 8 * (o % 2) + 8)
                    nm = nmax[:, s, :, hs]
                    to = [qs[:, s, :, MCOL + c].rearrange("p (t h) -> p t h", t=2)[:, :, hs] for c in range(3)]
                    pool.tensor_copy(to[0], nm).then_inc(nm_done.sem, 1)
                    pool.wait_ge(nm_done.sem, nm_done.of(i, 4 * o + 1))
                    pool.tensor_tensor(nme[:], nm, to[0], ALU.subtract).then_inc(nm_done.sem, 1)
                    pool.wait_ge(nm_done.sem, nm_done.of(i, 4 * o + 2))
                    pool.sem_inc(pool_passed.sem, 1)
                    pool.tensor_copy(to[1], nme[:]).then_inc(nm_done.sem, 1)
                    pool.wait_ge(nm_done.sem, nm_done.of(i, 4 * o + 3))
                    pool.tensor_tensor(to[2], nme[:], to[1], ALU.subtract).then_inc(nm_done.sem, 1)

            walk(pool, POOL_ORDER, part)

        @block.scalar
        def _(sc):
            def part(k, i, name, w=None, c=None):
                if name == "lnx":
                    src = {"ffn1": x_in, "attn": x1, "gelu": u2, "ffn2": x2}[w]
                    by = lnr if w == "attn" else rstd[w]
                    if w == "ffn1":
                        sc.wait_ge(xt_done["attn"].sem, xt_done["attn"].of(i - 1))
                    sc.wait_ge(rs_done[w].sem, rs_done[w].of(i))
                    for t in range(NT):
                        ins = sc.activation(xn[SIDE[w]][:, t], src[:, t], ACT.Identity, bias=shift[w][:, t:t + 1],
                                            scale=by[:, t:t + 1])
                    ins.then_inc(xn_done[w].sem, 1)
                elif name == "lnh":
                    sc.wait_ge(xt_done[w].sem, xt_done[w].of(i))
                    src = bd[D_AT["lnT", w]]
                    if w == "attn":
                        sc.wait_ge(qkv_full.sem, qkv_full.of(i - 1))
                        if is_first(i):
                            sc.wait_ge(loaded.sem, 16 * len(LOADS))
                    for to in (full[w], hT[w][0]):
                        if w in FFN:
                            ins = sc.activation(to[:], src[:], ACT.Copy)
                        else:
                            at = 0 if w == "attn" else 2
                            ins = sc.activation(to[:], src[:], ACT.Identity, bias=cols[:, at + 1:at + 2], scale=cols[:, at:at + 1])
                    ins.then_inc(ht_done[w].sem, 1)
                elif name == "tanh":
                    if c >= 2:
                        sc.wait_ge(sg_done[w].sem, sg_done[w].of(i, c - 1))
                    sc.wait_ge(gate_done[w].sem, gate_done[w].of(i, c + 1))
                    sc.activation(th[SIDE[w]][:, c % 2], bd[D_AT["gate", w, c]][:], ACT.Tanh, scale=0.5).then_inc(tanh_done[w].sem, 1)
                elif name == "stkx":
                    sc.wait_ge(max_full.sem, max_full.of(i - 1, 12 * w + 12))
                    sc.wait_ge(stk_full.sem, stk_full.of(i, 4 * w + c + 1))
                    sc.activation(qT[:, w, 4 * (c // 2):4 * (c // 2) + 4],
                                  bx[X_AT["stk", w, c]][:].bitcast(BF16).rearrange("p (h t) -> p h t", h=4), ACT.Copy)\
                        .then_inc(qt_done.sem, 1)
                elif name == "oTx":
                    sc.wait_ge(ot_tr.sem, ot_tr.of(i))
                    sc.activation(oT[:], bd[D_AT["oT",]][:], ACT.Copy).then_inc(ot_done.sem, 1)
                elif name == "gelu":
                    sc.wait_ge(w1_done.sem, w1_done.of(i, w + 1))
                    sc.activation(act[BACK][:, w], bd[D_AT["w1", w]][:], ACT.Gelu, bias=cols[:, 4 + w:5 + w]).then_inc(gelu_done.sem, 1)
                elif name == "p1":
                    sc.wait_ge(stack_done.sem, stack_done.of(i, w))
                    sc.wait_ge(r_done.sem, r_done.of(i, 2 * w + 2))
                    sc.activation(part1[:], r[:], ACT.Copy).then_inc(p1_done.sem, 1)
                elif name == "p2":
                    sc.wait_ge(e1_done.sem, e1_done.of(i, w + 1))
                    sc.activation(part2[:], e1[:], ACT.Copy).then_inc(p2_done.sem, 1)
                elif name == "exp":
                    n = 3 * w + c
                    sc.wait_ge(pv_done.sem, pv_done.of(i, w - 1))
                    sc.wait_ge(m_full.sem, m_full.of(i, n + 1))
                    sc.activation(pT[:, w % 2, c], bm[n % 2][:], ACT.Exp, scale=HD ** -0.5).then_inc(m_free.sem, 1)
                elif name == "oq":
                    sc.wait_ge(pv_done.sem, pv_done.of(i, w + 1))
                    sc.activation(oq[:], bo[:, 0:T], ACT.Copy).then_inc(oq_done.sem, 1)
                elif name == "hand":
                    sc.wait_ge(u_done.sem, u_done.of(i))
                    sc.wait_ge(u2_done.sem, u2_done.of(i - 1))
                    sc.wait_ge(ux_done.sem, ux_done.of(i - 1))
                    sc.activation(u_back[:], u[:], ACT.Copy)
                    sc.activation(x1b_back[:], x1b[:], ACT.Copy).then_inc(handed.sem, 1)

            walk(sc, SC_ORDER, part)

        @block.tensor
        def _(pe):
            pe.wait_ge(ffn_loaded.sem, 16 * len(FFN_LOADS))
            pe.wait_ge(split_done.sem, 4)

            def three_products(to, still, moving):
                pe.matmul(to, still[0], moving[0], start=True, stop=False)
                pe.matmul(to, still[1], moving[0], start=False, stop=False)
                return pe.matmul(to, still[0], moving[1], start=False, stop=True)

            released = {
                "oT": lambda i: (ot_done.sem, ot_done.of(i)), "wo": lambda i: (u2_done.sem, u2_done.of(i)),
                "lnT": lambda i, b: (ht_done[b].sem, ht_done[b].of(i)), "w1": lambda i, c: (gelu_done.sem, gelu_done.of(i, c + 1)),
                "w2": lambda i: (x2_done.sem, x2_done.of(i)), "gate": lambda i, b, c: (sg_done[b].sem, sg_done[b].of(i, c + 1)),
                "up": lambda i, b, c: (mul_done[b].sem, mul_done[b].of(i, c + 1)),
                "down": lambda i, b: (x1_done.sem, x1_done.of(i)) if b == "ffn1" else (out_done.sem, out_done.of(i)),
                "qkv": lambda i, s, t: (vs_done.sem, vs_done.of(i, 2 * s + t + 1)),
                "stk": lambda i, s, b: ((kt_done, qt_done)[b % 2].sem, (kt_done, qt_done)[b % 2].of(i, 2 * s + b // 2 + 1)),
                "max": lambda i, g, b: (mx_done.sem, mx_done.of(i, 3 * g + b + 1)),
                "q2T": lambda i, o: (q2x_done.sem, q2x_done.of(i, o + 1)),
            }

            def bank_free(k, part):
                user = before(k, part)
                if user is None:
                    return ffn_loaded.sem, 0
                (name, *which), pair = user
                return released[name](pair, *which)

            def part(k, i, name, w=None, c=None):
                if name == "lnT":
                    pe.wait_ge(*bank_free(k, (name, w)))
                    pe.wait_ge(xn_done[w].sem, xn_done[w].of(i))
                    to = bd[D_AT[name, w]]
                    for t in range(NT):
                        mm = pe.transpose(to[:, t * P:(t + 1) * P], xn[SIDE[w]][:, t], ident[:])
                    mm.then_inc(xt_done[w].sem, 1)
                elif name in ("gate", "up"):
                    pe.wait_ge(*bank_free(k, (name, w, c)))
                    pe.wait_ge(lo_done[w].sem, lo_done[w].of(i))
                    weight, done = (wgate, gate_done) if name == "gate" else (wup, up_done)
                    three_products(bd[D_AT[name, w, c]][:], [z[:, c * P:(c + 1) * P] for z in weight], [z[:] for z in hT[w]])\
                        .then_inc(done[w].sem, 1)
                elif name == "down":
                    if is_first(i):
                        pe.wait_ge(scaled_done.sem, 1)
                    pe.wait_ge(*bank_free(k, (name, w)))
                    pe.wait_ge(mul_done[w].sem, mul_done[w].of(i))
                    to = bd[D_AT[name, w]]
                    for t in range(NT):
                        for n in range(CH):
                            mm = pe.matmul(to[:, t * D:(t + 1) * D], act[SIDE[w]][:, n, t * P:(t + 1) * P], wdown[:, n],
                                           start=(n == 0), stop=(n == CH - 1))
                    mm.then_inc(down_done[w].sem, 1)
                elif name == "oT":
                    pe.wait_ge(*bank_free(k, (name,)))
                    pe.wait_ge(on_done.sem, on_done.of(i))
                    to = bd[D_AT[name,]]
                    for t in range(NT):
                        mm = pe.transpose(to[:, t * P:(t + 1) * P], on[:, t], ident[:])
                    mm.then_inc(ot_tr.sem, 1)
                elif name == "wo":
                    if is_first(i):
                        pe.wait_ge(scaled_done.sem, 4)
                    pe.wait_ge(*bank_free(k, (name,)))
                    pe.wait_ge(ot_done.sem, ot_done.of(i))
                    to = bd[D_AT[name,]]
                    for t in range(NT):
                        mm = pe.matmul(to[:, t * D:(t + 1) * D], oT[:, t * P:(t + 1) * P], wo[:], start=True, stop=True)
                    mm.then_inc(wo_done.sem, 1)
                elif name == "w1":
                    pe.wait_ge(*bank_free(k, (name, w)))
                    pe.wait_ge(lo_done["gelu"].sem, lo_done["gelu"].of(i))
                    three_products(bd[D_AT[name, w]][:], [z[:, w * P:(w + 1) * P] for z in w12], [z[:] for z in hT["gelu"]])\
                        .then_inc(w1_done.sem, 1)
                elif name == "w2":
                    pe.wait_ge(*bank_free(k, (name,)))
                    pe.wait_ge(gelu_done.sem, gelu_done.of(i))
                    to = bd[D_AT[name,]]
                    for t in range(NT):
                        for n in range(CF):
                            mm = pe.matmul(to[:, t * D:(t + 1) * D], act[BACK][:, n, t * P:(t + 1) * P], w2[:, n],
                                           start=(n == 0), stop=(n == CF - 1))
                    mm.then_inc(w2_done.sem, 1)
                elif name == "qkv":
                    if is_first(i):
                        pe.wait_ge(split_done.sem, 8)
                    pe.wait_ge(*bank_free(k, (name, w, c)))
                    pe.wait_ge(lo_done["attn"].sem, lo_done["attn"].of(i))
                    at = (2 * w + c) * P
                    three_products(bx[X_AT[name, w, c]][:, 0:3 * D], [z[:, at:at + P] for z in hT["attn"]], [z[:] for z in wqkv2])\
                        .then_inc(qkv_full.sem, 1)
                elif name == "stk":
                    if is_first(i):
                        pe.wait_ge(loaded.sem, 16 * len(LOADS))
                    pe.wait_ge(stack_done.sem, stack_done.of(i, w + 1))
                    pe.wait_ge(nm_clear.sem, nm_clear.of(i, w + 1))
                    pe.wait_ge(*bank_free(k, (name, w, c)))
                    to = bx[X_AT[name, w, c]][:].bitcast(BF16)
                    src = (ks, qs)[c % 2]
                    for h2 in range(4):
                        for t in range(2):
                            at = t * H + 8 * (c // 2) + 2 * h2
                            mm = pe.transpose(to[:, h2 * T + t * P:h2 * T + (t + 1) * P],
                                              src[:, w, at:at + 2].rearrange("p h c -> p (h c)"), identb[:])
                    mm.then_inc(stk_full.sem, 1)
                elif name == "max":
                    s, heads, rows_h = heads_of(w)
                    heads = range(H)[heads]
                    pe.wait_ge(kt_done.sem, kt_done.of(i, w // 2 + 1))
                    pe.wait_ge(qt_done.sem, qt_done.of(i, w // 2 + 1))
                    pe.wait_ge(*bank_free(k, (name, w, c)))
                    to = bx[X_AT[name, w, c]]
                    tile = min(c, 1)
                    n = P if tile == 0 else T
                    for at, h in enumerate(heads if tile == 0 else heads[2 * (c - 1):2 * c]):
                        mm = pe.matmul(to[:, at * n:(at + 1) * n], qT[rows_h, s, h // 2, tile * P:(tile + 1) * P],
                                       kT[rows_h, s, h // 2, 0:n], start=True, stop=True)
                    mm.then_inc(max_full.sem, 1)
                elif name == "q2T":
                    s = w // 2
                    pe.wait_ge(nm_done.sem, nm_done.of(i, 4 * w + 4))
                    pe.wait_ge(*bank_free(k, (name, w)))
                    to = bx[X_AT[name, w]][:].bitcast(BF16)
                    for h2 in range(4):
                        for t in range(2):
                            at = t * H + 8 * (w % 2) + 2 * h2
                            mm = pe.transpose(to[:, h2 * T + t * P:h2 * T + (t + 1) * P],
                                              qs[:, s, at:at + 2].rearrange("p h c -> p (h c)"), identb[:])
                    mm.then_inc(q2t_full.sem, 1)
                elif name == "main":
                    s, heads, rows_h = heads_of(w)
                    heads = range(H)[heads]
                    pe.wait_ge(q2x_done.sem, q2x_done.of(i, w // 2 + 1))
                    n = 3 * w + c
                    if n >= 2:
                        pe.wait_ge(m_free.sem, m_free.of(i, n - 1))
                    else:
                        pe.wait_ge(m_free.sem, m_free.of(i - 1, m_free.per + n - 1))
                    to = bm[n % 2]
                    tile = c // 2
                    n = T if tile == 0 else P
                    pe.matmul(to[:], identb[:], mask_main[:, tile], start=True, stop=False, skip_group_check=True)
                    for at, h in enumerate(heads if tile == 1 else heads[2 * c:2 * c + 2]):
                        mm = pe.matmul(to[:, at * n:(at + 1) * n], kT[rows_h, s, h // 2, tile * P:(tile + 1) * P],
                                       q2T[rows_h, w // 2 % 2, h % 8 // 2, T - n:T], start=False, stop=True,
                                       skip_group_check=True)
                    mm.then_inc(m_full.sem, 1)
                elif name == "pv":
                    if is_first(i):
                        pe.wait_ge(stacks_set.sem, 4)
                    s, heads, _ = heads_of(w)
                    pe.wait_ge(m_free.sem, m_free.of(i, 3 * w + 3))
                    pe.wait_ge(on_done.sem, on_done.of(i, w))
                    for n, h in enumerate(range(H)[heads]):
                        pe.matmul(bo[32 * n:32 * n + 32, 0:T], vs[:, s, h],
                                  pT[:, w % 2, n // 2, (n % 2) * T:(n % 2 + 1) * T], start=True, stop=False, skip_group_check=True)
                    for n, h in enumerate(range(H)[heads]):
                        mm = pe.matmul(bo[32 * n:32 * n + 32, P:T], vs[:, s, H + h],
                                       pT[:, w % 2, 2, n * P:(n + 1) * P], start=False, stop=True, skip_group_check=True)
                    mm.then_inc(pv_done.sem, 1)
                elif name == "oqT":
                    pe.wait_ge(oq_done.sem, oq_done.of(i, w + 1))
                    for t in range(2):
                        mm = pe.transpose(bo[:, T + t * P:T + (t + 1) * P], oq[:, t * P:(t + 1) * P], ident[:])
                    mm.then_inc(oqt_done.sem, 1)

            walk(pe, PE_ORDER, part)

        @block.vector
        def _(ve):
            def split(weight, halves, at):
                ve.tensor_copy(halves[0][:], weight).then_inc(split_done.sem, 1)
                ve.wait_ge(split_done.sem, at + 1)
                ve.tensor_tensor(halves[1][:], weight, halves[0][:].bitcast(F32), ALU.subtract).then_inc(split_done.sem, 1)

            ve.memset(qs[:], 0.0).then_inc(stacks_set.sem, 1)
            ve.wait_ge(ffn_loaded.sem, 16 * len(FFN_LOADS))
            ve.tensor_scalar(dequantised[:, 0], gate_i[:], SCALE, None, ALU.mult).then_inc(dequant_done.sem, 1)
            ve.tensor_scalar(dequantised[:, 1], up_i[:], SCALE, 0.5, ALU.mult, ALU.mult).then_inc(dequant_done.sem, 1)

            def ffn_weights():
                ve.wait_ge(dequant_done.sem, 2)
                split(dequantised[:, 0], wgate, 0)
                split(dequantised[:, 1], wup, 2)

            def other_weights():
                ve.wait_ge(loaded.sem, 16 * len(LOADS))
                ve.tensor_scalar(wdown[:].rearrange("p c d -> p (c d)"), down_i[:], SCALE, 0.5, ALU.mult, ALU.mult)\
                    .then_inc(scaled_done.sem, 1)
                split(w1[:], w12, 4)
                split(wqkv[:], wqkv2, 6)
                ve.tensor_tensor(wo[:], wo[:], rows[:, 0], ALU.mult).then_inc(scaled_done.sem, 1)
                for c in range(CF):
                    ins = ve.tensor_tensor(w2[:, c], w2[:, c], rows[:, 1], ALU.mult)
                ins.then_inc(scaled_done.sem, 1)
                ve.tensor_tensor(b2l[:], rows[:, 2], rows[:, 1], ALU.mult).then_inc(scaled_done.sem, 1)
                ve.wait_ge(stacks_set.sem, 4)

            def part(k, i, name, w=None, c=None):
                if name == "stat":
                    src, ready = {"ffn1": (x_in, x_loaded), "attn": (x1, x1_done),
                                  "gelu": (u2, u2_done), "ffn2": (x2, x2_done)}[w]
                    ve.wait_ge(ready.sem, ready.of(i))
                    for t in range(NT):
                        ins = ve.bn_stats(stats[w][:, t], src[:, t])
                    ins.then_inc(bn_done[w].sem, 1)
                    if w == "attn":
                        ve.wait_ge(u_done.sem, u_done.of(i - 1))
                    ve.wait_ge(bn_done[w].sem, bn_done[w].of(i))
                    ve.sem_inc(vector_passed.sem, 1)
                    for t in range(NT):
                        ins = ve.bn_aggr(mv[w][:, t], stats[w][:, t])
                    ins.then_inc(mv_done[w].sem, 1)
                    if is_first(i) and w == "ffn1":
                        ffn_weights()
                elif name == "sg":
                    if is_first(i) and w == "ffn1" and c == 0:
                        other_weights()
                    ve.wait_ge(tanh_done[w].sem, tanh_done[w].of(i, c + 1))
                    ve.scalar_tensor_tensor(sg[SIDE[w]][:, c % 2], th[SIDE[w]][:, c % 2], 1.0, bd[D_AT["gate", w, c]][:],
                                            ALU.add, ALU.mult).then_inc(sg_done[w].sem, 1)
                elif name == "mul":
                    ve.wait_ge(sg_done[w].sem, sg_done[w].of(i, c + 1))
                    ve.wait_ge(up_done[w].sem, up_done[w].of(i, c + 1))
                    ve.tensor_tensor(act[SIDE[w]][:, c], sg[SIDE[w]][:, c % 2], bd[D_AT["up", w, c]][:], ALU.mult)\
                        .then_inc(mul_done[w].sem, 1)
                elif name == "res":
                    y = bd[D_AT["down", w]][:].rearrange("p (t d) -> p t d", t=NT)
                    if w == "ffn1":
                        ve.wait_ge(u_done.sem, u_done.of(i - 1))
                        ve.wait_ge(down_done[w].sem, down_done[w].of(i))
                        ve.tensor_tensor(x1[:], x_in[:], y, ALU.add).then_inc(x1_done.sem, 1)
                    else:
                        ve.wait_ge(out_stored.sem, out_stored.of(i - 1))
                        ve.wait_ge(down_done[w].sem, down_done[w].of(i))
                        ve.tensor_tensor(xout[:], x2[:], y, ALU.add).then_inc(out_done.sem, 1)
                elif name == "u2":
                    ve.wait_ge(handed.sem, handed.of(i))
                    ve.wait_ge(ux_done.sem, ux_done.of(i - 1))
                    ve.wait_ge(wo_done.sem, wo_done.of(i))
                    ve.tensor_tensor(u2[:], u_back[:], bd[D_AT["wo",]][:].rearrange("p (t d) -> p t d", t=NT), ALU.add)\
                        .then_inc(u2_done.sem, 1)
                elif name == "x2":
                    ve.wait_ge(ux_done.sem, ux_done.of(i))
                    ve.wait_ge(w2_done.sem, w2_done.of(i))
                    ve.tensor_tensor(x2[:], ux[:], bd[D_AT["w2",]][:].rearrange("p (t d) -> p t d", t=NT), ALU.add)\
                        .then_inc(x2_done.sem, 1)
                elif name == "rot":
                    if w == 1:
                        ve.wait_ge(r_done.sem, r_done.of(i, c + 1))
                    else:
                        ve.wait_ge(r_done.sem, r_done.of(i - 1, 3 + c))
                    ve.wait_ge(pv_done.sem, pv_done.of(i - 1, 4 * w + 4))
                    ve.wait_ge(qkv_full.sem, qkv_full.of(i, 2 * w + c + 1))
                    src = bx[X_AT["qkv", w, c]]
                    ve.tensor_tensor(rot1[:, c], src[:, 0:2 * D], cosr[:, c], ALU.mult)
                    for half in range(2):
                        def cut(ap, k):
                            return ap.rearrange("p (h c) -> p h c", c=HD)[:, :, HD // 2 * k:HD // 2 * (k + 1)]
                        ins = ve.tensor_tensor(cut(rot2[:, c], half), cut(src[:, 0:2 * D], 1 - half),
                                               cut(sinr[:, c], half), ALU.mult)
                    ins.then_inc(rot_done.sem, 1)
                    ve.tensor_copy(vs[:, w, c * H:(c + 1) * H, 0:HD],
                                   src[:, 2 * D:3 * D].rearrange("p (h c) -> p h c", c=HD)).then_inc(vs_done.sem, 1)
                elif name == "stack":
                    ve.wait_ge(p3_done.sem, p3_done.of(i, w + 1))
                    ve.wait_ge(q2t_full.sem, q2t_full.of(i - 1, 2 * w + 2))
                    q1, q2, q3 = (z[:, 0].rearrange("p (h c) -> p h c", c=HD) for z in (part1, part2, part3))
                    k1, k2, k3 = (z[:, 1].rearrange("p (h c) -> p h c", c=HD) for z in (part1, part2, part3))
                    for at, z in ((0, q1), (8, q1), (16, q1), (24, q3), (40, q2), (48, q2)):
                        ve.tensor_copy(qs[:, w, :, at:at + HD], z)
                    for at, z in ((0, k1), (8, k2), (16, k3), (24, k1), (40, k1), (48, k2)):
                        ins = ve.tensor_copy(ks[:, w, :, at:at + HD], z)
                    ins.then_inc(stack_done.sem, 1)
                elif name == "stkx":
                    ve.wait_ge(m_full.sem, m_full.of(i - 1, 12 * w + 12))
                    ve.wait_ge(stk_full.sem, stk_full.of(i, 4 * w + c + 1))
                    ve.tensor_copy(kT[:, w, 4 * (c // 2):4 * (c // 2) + 4],
                                   bx[X_AT["stk", w, c]][:].bitcast(BF16).rearrange("p (h t) -> p h t", h=4)).then_inc(kt_done.sem, 1)
                elif name == "mx":
                    s, heads, _ = heads_of(w)
                    heads = range(H)[heads]
                    n = 3 * w + c
                    src = bx[X_AT["max", w, c]]
                    ve.wait_ge(nm_done.sem, nm_done.of(i - 1, 4 * (w // 2) + 4))
                    ve.wait_ge(mx_done.sem, mx_done.of(i, n - 1))
                    ve.wait_ge(max_full.sem, max_full.of(i, n + 1))
                    ve.sem_inc(vector_passed.sem, 1)
                    tile = min(c, 1)
                    wide = P if tile == 0 else T
                    for at, h in enumerate(heads if tile == 0 else heads[2 * (c - 1):2 * c]):
                        ins = ve.tensor_tensor_reduce(masked[:, n % 2, at * wide:(at + 1) * wide], src[:, at * wide:(at + 1) * wide],
                                                      mask_max[:, tile, 0:wide], -1.0, -2 * MASKED, ALU.add, ALU.min,
                                                      nmax[:, s, tile, h:h + 1])
                    ins.then_inc(mx_done.sem, 1)
                elif name == "q2x":
                    if w >= 2:
                        ve.wait_ge(m_full.sem, m_full.of(i, 6 * (w - 1)))
                    else:
                        ve.wait_ge(m_full.sem, m_full.of(i - 1, 6 * (w + 3)))
                    ve.wait_ge(q2t_full.sem, q2t_full.of(i, w + 1))
                    ve.tensor_copy(q2T[:, w % 2], bx[X_AT["q2T", w]][:].bitcast(BF16).rearrange("p (h t) -> p h t", h=4))\
                        .then_inc(q2x_done.sem, 1)
                elif name == "norm":
                    s, heads, _ = heads_of(w)
                    ve.wait_ge(oqt_done.sem, oqt_done.of(i, w + 1))
                    y = bo[:, T:2 * T].rearrange("p (h c) -> p h c", c=32)
                    ve.reciprocal(rden[:], y[:, :, HD]).then_inc(rden_done.sem, 1)
                    ve.wait_ge(ot_tr.sem, ot_tr.of(i - 1))
                    ve.wait_ge(rden_done.sem, rden_done.of(i, w + 1))
                    ve.tensor_tensor(on[:, 2 * s:2 * s + 2].rearrange("p t (h c) -> p t h c", c=HD)[:, :, heads],
                                     bo[:, T:2 * T].rearrange("p (t h c) -> p t h c", t=2, c=32)[:, :, :, 0:HD],
                                     rden[:].rearrange("p (t h) -> p t h", t=2).unsqueeze(3).to_broadcast([P, 2, QUAD, HD]),
                                     ALU.mult).then_inc(on_done.sem, 1)

            walk(ve, VE_ORDER, part)


_OUT = (B, T, D)


def constants():
    f = np.float32
    inv = (f(1.0) / np.power(f(10000.0), np.arange(0, HD, 2, dtype=f) / f(HD))).astype(f)
    ang = np.outer(np.arange(T, dtype=f), inv).astype(f)
    cos, sin = np.cos(ang).astype(f), np.sin(ang).astype(f)
    cos = np.tile(np.concatenate([cos, cos], 1), (1, 2 * H)).reshape(2, P, 2 * D).transpose(1, 0, 2)
    sin = np.tile(np.concatenate([-sin, sin], 1), (1, 2 * H)).reshape(2, P, 2 * D).transpose(1, 0, 2)
    t, s = np.arange(T)[:, None], np.arange(T)[None, :]
    ok = (t >= s) & (t - s < WINDOW)
    m = np.where(ok, f(0), f(MASKED))
    bf = mybir.dt.np(BF16)
    mask_max = m.reshape(2, P, T).transpose(1, 0, 2)
    mask_main = np.stack([np.tile(m.T[:P], (1, 2)), np.tile(m.T[P:, P:], (1, 4))], 1).astype(bf)
    return {"cos": cos, "sin": sin, "ident": np.eye(P, dtype=f), "identb": np.eye(P).astype(bf),
            "mask_max": mask_max, "mask_main": mask_main}


def kernel(**inputs):
    import concourse.bacc as _bacc
    from concourse.bass_utils import run_bass_kernel_spmd as _run

    z = {k.removeprefix("L0_attn_").removeprefix("L0_ffn_"): np.asarray(v) for k, v in inputs.items()}
    arrays = constants()
    arrays["x"] = z["x"].reshape(B * T, D)
    arrays["wqkv"] = np.concatenate([z["wq"].T, z["wk"].T, z["wv"].T], 1)
    arrays["wo"] = z["wo"].T
    arrays["w1"] = z["w1"].T
    arrays["w2"] = z["w2"].T.reshape(CF, P, D).transpose(1, 0, 2)
    arrays["w_gate"] = z["w_gate"].T
    arrays["w_up"] = z["w_up"].T
    arrays["w_down"] = z["w_down"].T.reshape(CH, P, D).transpose(1, 0, 2).reshape(P, CH * D)
    arrays["cols"] = np.concatenate([z[n].reshape(P, 1) for n in ("norm1_w", "norm1_b", "norm2_w", "norm2_b")]
                                    + [z["b1"].reshape(CF, P).T], 1)
    arrays["rows"] = np.broadcast_to(np.stack([z["ls1"], z["ls2"], z["b2"]])[None], (P, 3, D))
    nc = _bacc.Bacc("TRN2", target_bir_lowering=False, num_devices=1)
    arrays = {f"in_{k}": np.ascontiguousarray(v) for k, v in arrays.items()}
    aps = {k[3:]: nc.dram_tensor(k, v.shape, mybir.dt.from_np(v.dtype), kind="ExternalInput").ap() for k, v in arrays.items()}
    aps["out"] = nc.dram_tensor("out_y", (B * T, D), F32, kind="ExternalOutput").ap()
    build(nc, aps)
    res = _run(nc, [arrays], core_ids=[0])
    return res.results[0]["out_y"].reshape(_OUT)
```
